# Optimizing a Trainium2 kernel written in Bass

```python
import numpy as np
import jax
import jax.numpy as jnp

def _softmax(x, axis=-1):
    return jax.nn.softmax(x, axis=axis)

def _gelu(x):
    return jax.nn.gelu(x, approximate=True)

def _silu(x):
    return jax.nn.silu(x)

def _sigmoid(x):
    return jax.nn.sigmoid(x)

def _layernorm(x, axis=-1, eps=1e-05):
    m = jnp.mean(x, axis=axis, keepdims=True)
    v = jnp.var(x, axis=axis, keepdims=True)
    return (x - m) / jnp.sqrt(v + eps)

def _scatter_add(tgt, idx, src, axis=0):
    return tgt.at[idx].add(src)

def _segment_sum(src, seg, n):
    return jax.ops.segment_sum(src, seg, n)
kernel_name = 'mk_cond_resid_d2_seqx_r4_6cd693'

def setup_inputs(seed: int=0):
    np.random.seed(seed)
    _w = jnp.asarray

    def _rec_inputs():
        import jax
        import jax.numpy as jnp
        _rk = jax.random.key(seed)
        x = 7.22e-05 + 1 * jax.random.normal(jax.random.fold_in(_rk, 1), (8, 256, 256), jnp.float32)
        _lenS = 256 - jax.random.randint(jax.random.fold_in(_rk, 7), (8,), 0, max(1, 256 // 4) + 1, jnp.int32)
        _lenS2 = 256 - jax.random.randint(jax.random.fold_in(_rk, 8), (8,), 0, max(1, 256 // 4) + 1, jnp.int32)
        fside_BxSxS_0 = 4.13588e-05 + 0.999923 * jax.random.normal(jax.random.fold_in(_rk, 11), (8, 256, 256), jnp.float32)
        itok_B_18_1004 = jax.random.randint(jax.random.fold_in(_rk, 12), (8,), 18, 1005, jnp.int32)
        itok_B_0_2 = jax.random.randint(jax.random.fold_in(_rk, 13), (8,), 0, 3, jnp.int32)
        return (x, fside_BxSxS_0, itok_B_18_1004, itok_B_0_2)
    x, fside_BxSxS_0, itok_B_18_1004, itok_B_0_2 = _rec_inputs()

    def _L0_cond_setup():
        import jax, jax.numpy as jnp
        import numpy as np
        B, L1, L2, DIN, DOUT, H = (8, 256, 256, 256, 256, 16)
        DH = DOUT // H
        SCALE = 1.0 / np.sqrt(DH).astype(np.float32)
        key = jax.random.key(seed)
        ks = jax.random.split(key, 13)
        s = 0.02
        return {'seq1': jax.random.normal(ks[0], (B, L1, DIN), jnp.float32), 'seq2': jax.random.normal(ks[1], (B, L2, DIN), jnp.float32), 'seq_len1': jax.random.randint(ks[2], (B,), 1, L1 + 1, jnp.int32), 'Wq': jax.random.normal(ks[3], (DIN, DOUT), jnp.float32) * s, 'bq': jnp.zeros((DOUT,), jnp.float32), 'Wk': jax.random.normal(ks[4], (DIN, DOUT), jnp.float32) * s, 'bk': jnp.zeros((DOUT,), jnp.float32), 'Wv': jax.random.normal(ks[5], (DIN, DOUT), jnp.float32) * s, 'bv': jnp.zeros((DOUT,), jnp.float32), 'Wo': jax.random.normal(ks[6], (DOUT, DOUT), jnp.float32) * s, 'bo': jnp.zeros((DOUT,), jnp.float32), 'b_prev': jax.random.normal(ks[7], (1, 1, DIN), jnp.float32) * s, 'b_self': jax.random.normal(ks[8], (1, 1, DIN), jnp.float32) * s}
    _L0_cond_all = _L0_cond_setup()
    _L0_cond_in = {k: v for k, v in _L0_cond_all.items() if k in ('Wq', 'bq', 'Wk', 'bk', 'Wv', 'bv', 'Wo', 'bo', 'b_prev', 'b_self')}
    del _L0_cond_all

    def _L1_cond_setup():
        import jax, jax.numpy as jnp
        import numpy as np
        NEG_INF = -1e+30
        key = jax.random.key(seed)
        k1, k2, k3, k4, k5 = jax.random.split(key, 5)
        B, S, D, A = (16, 256, 256, 64)
        hidden = jax.random.normal(k1, (B, S, D), dtype=jnp.float32)
        W1 = jax.random.normal(k2, (D, A), dtype=jnp.float32) / np.sqrt(D)
        b1 = jax.random.normal(k3, (A,), dtype=jnp.float32) * 0.01
        v = jax.random.normal(k4, (A,), dtype=jnp.float32) / np.sqrt(A)
        prompt_type_ids = jax.random.randint(k5, (B,), 0, 3, dtype=jnp.int32)
        return {'hidden': hidden, 'W1': W1, 'b1': b1, 'v': v, 'prompt_type_ids': prompt_type_ids}
    _L1_cond_all = _L1_cond_setup()
    _L1_cond_in = {k: v for k, v in _L1_cond_all.items() if k in ('W1', 'b1', 'v')}
    del _L1_cond_all
    return {'x': x, 'fside_BxSxS_0': fside_BxSxS_0, 'itok_B_18_1004': itok_B_18_1004, 'itok_B_0_2': itok_B_0_2, 'L0_cond_Wq': _L0_cond_in['Wq'], 'L0_cond_bq': _L0_cond_in['bq'], 'L0_cond_Wk': _L0_cond_in['Wk'], 'L0_cond_bk': _L0_cond_in['bk'], 'L0_cond_Wv': _L0_cond_in['Wv'], 'L0_cond_bv': _L0_cond_in['bv'], 'L0_cond_Wo': _L0_cond_in['Wo'], 'L0_cond_bo': _L0_cond_in['bo'], 'L0_cond_b_prev': _L0_cond_in['b_prev'], 'L0_cond_b_self': _L0_cond_in['b_self'], 'L1_cond_W1': _L1_cond_in['W1'], 'L1_cond_b1': _L1_cond_in['b1'], 'L1_cond_v': _L1_cond_in['v']}

def reference(x, fside_BxSxS_0, itok_B_18_1004, itok_B_0_2, L0_cond_Wq, L0_cond_bq, L0_cond_Wk, L0_cond_bk, L0_cond_Wv, L0_cond_bv, L0_cond_Wo, L0_cond_bo, L0_cond_b_prev, L0_cond_b_self, L1_cond_W1, L1_cond_b1, L1_cond_v):
    import jax
    import jax.numpy as jnp

    def _L0_cond_ref(seq1, seq2, seq_len1, Wq, bq, Wk, bk, Wv, bv, Wo, bo, b_prev, b_self):
        import jax, jax.numpy as jnp
        import numpy as np
        B, L1, L2, DIN, DOUT, H = (8, 256, 256, 256, 256, 16)
        DH = DOUT // H
        SCALE = 1.0 / np.sqrt(DH).astype(np.float32)
        b, l1, _ = seq1.shape
        l2 = seq2.shape[1]
        query = seq2 + b_self
        key = jnp.concatenate([seq1 + b_prev, seq2 + b_self], 1)
        value = jnp.concatenate([seq1, seq2], 1)
        q = (query @ Wq + bq).reshape(b, l2, H, DH).transpose(0, 2, 1, 3)
        k = (key @ Wk + bk).reshape(b, l1 + l2, H, DH).transpose(0, 2, 1, 3)
        v = (value @ Wv + bv).reshape(b, l1 + l2, H, DH).transpose(0, 2, 1, 3)
        score_prev = jnp.einsum('bhqd,bhkd->bhqk', q, k[:, :, :l1]) * SCALE
        score_self = (q * k[:, :, l1:]).sum(-1, keepdims=True) * SCALE
        mask = jnp.arange(l1)[None, :] < seq_len1[:, None]
        score_prev = jnp.where(mask[:, None, None, :], score_prev, -jnp.inf)
        score = jnp.concatenate([score_prev, score_self], -1)
        weights = jax.nn.softmax(score, axis=-1)
        attn = jnp.einsum('bhqk,bhkd->bhqd', weights[..., :-1], v[:, :, :l1])
        attn = attn + weights[..., -1:] * v[:, :, l1:]
        attn = attn.transpose(0, 2, 1, 3).reshape(b, l2, H * DH)
        return attn @ Wo + bo

    def _L1_cond_ref(hidden, W1, b1, v, prompt_type_ids):
        import jax, jax.numpy as jnp
        import numpy as np
        NEG_INF = -1e+30
        B, S, D = hidden.shape
        attn_in = jnp.tanh(jnp.einsum('bsd,da->bsa', hidden, W1) + b1)
        scores = jnp.einsum('bsa,a->bs', attn_in, v)
        idx = jnp.arange(S)
        j = idx[:, None]
        l = idx[None, :]
        prefix_m = l <= j
        postfix_m = l >= j
        cloze_m = l != j
        pt = prompt_type_ids[:, None, None]
        mask = jnp.where(pt == 0, prefix_m[None], jnp.where(pt == 1, postfix_m[None], cloze_m[None]))
        masked_scores = jnp.where(mask, scores[:, None, :], NEG_INF)
        p = jax.nn.softmax(masked_scores, axis=-1)
        cnt = jnp.sum(mask, axis=-1).astype(hidden.dtype)
        pooled = jnp.einsum('bjl,bld->bjd', p, hidden) / cnt[..., None]
        return pooled
    x = x + _L0_cond_ref(x, fside_BxSxS_0, itok_B_18_1004, L0_cond_Wq, L0_cond_bq, L0_cond_Wk, L0_cond_bk, L0_cond_Wv, L0_cond_bv, L0_cond_Wo, L0_cond_bo, L0_cond_b_prev, L0_cond_b_self)
    x = x + _L1_cond_ref(x, L1_cond_W1, L1_cond_b1, L1_cond_v, itok_B_0_2)
    return x

_drawn_inputs = setup_inputs


def setup_inputs(seed=0):
    import zlib

    import numpy as np

    out = dict(_drawn_inputs(seed))
    spreads = {'L0_cond_bq': (0.0, 0.8),
     'L0_cond_bk': (0.0, 2.0),
     'L0_cond_bv': (0.0, 0.975),
     'L0_cond_bo': (0.0, 0.1)}
    factors = {'fside_BxSxS_0': 8.0,
     'L0_cond_Wq': 8.0,
     'L0_cond_Wk': 8.0,
     'L0_cond_Wv': 6.575,
     'L0_cond_b_prev': 8.0,
     'L0_cond_b_self': 8.0,
     'L1_cond_W1': 4.599,
     'L1_cond_b1': 64.0,
     'L1_cond_v': 5.02}
    for name, (base, spread) in spreads.items():
        noise = np.random.default_rng([zlib.crc32(name.encode()), seed]).standard_normal(out[name].shape)
        drawn = base * np.exp(spread * noise) if base else spread * noise
        out[name] = jnp.asarray(drawn.astype(out[name].dtype))
    for name, factor in factors.items():
        out[name] = (out[name] * factor).astype(out[name].dtype)
    return out
```

```python
from contextlib import ExitStack

import concourse.bass as bass
from concourse import mybir

F32 = mybir.dt.float32
F32R = mybir.dt.float32r
I32 = mybir.dt.int32
ALU = mybir.AluOpType
ACT = mybir.ActivationFunctionType
AX = mybir.AxisListType

P = 128
MASKED = -1e30

SHARED = [
    ("TX", 1, ("xt_lo", 1)), ("TS", 1, ("st_lo", 1)),
    ("Z", -2, ("tanh_done", 1)), ("MT3", -1, ("mt_copied", 4)), ("Q", 1, ("q_copied", 1)),
    ("K", 1, ("k_copied", 1)),
    ("SB", -2, ("masked_done", 1)), ("KS", 1, ("prod_done", 1)),
    ("MT0", 0, ("mt_copied", 1)), ("SS", 1, ("ss_copied", 1)),
    ("PT", -2, ("pt_copied", 1)),
    ("PO", -2, ("out_done", 1)),
    ("MT1", 0, ("mt_copied", 2)), ("V", 1, ("v_copied", 1)),
    ("NAT0", -1, ("num_done", 1)), ("NAT1", -1, ("num_done", 2)),
    ("VS", 1, ("vs_copied", 1)),
    ("AT", -1, ("at_lo", 1)),
    ("MT2", 0, ("mt_copied", 3)), ("WO", -1, ("x1_done", 1)),
    ("X1T", -1, ("x1t_copied", 1)),
]
PER_BATCH = {"mt_copied": 4, "num_done": 2}


def build(nc, x, side, seq_len, kind, Wq, bq, Wk, bk, Wv, bv, Wo, bo, b_prev, b_self, W1, b1, v, out):
    B, S, D = x.shape
    DH = 16
    H = D // DH
    NJ = H // 2
    KB = D // P
    A = W1.shape[1]
    ROWS = 3 * DH
    R_MASK, R_MAX = ROWS, ROWS + 1
    KM = ROWS + 1
    KF = ROWS + 3
    SLOTS = H
    LAG = 8
    GRP = 4
    NG = H // GRP
    QSCALE = 1.0 / DH ** 0.5
    assert (S, D, H, KB, SLOTS) == (256, 256, 16, 2, 16)

    with ExitStack() as ctx:
        def sb(name, shape, dt=F32):
            return ctx.enter_context(nc.sbuf_tensor(name, shape, dt))

        def ps(name, shape):
            return ctx.enter_context(nc.psum_tensor(name, shape, F32))

        sems = {}

        def sem(name):
            sems[name] = ctx.enter_context(nc.semaphore(name))
            return sems[name]

        ps_max = ps("ps_max", [P, 2, KB, S])
        ps_exp = ps("ps_exp", [P, 2, KB, S])
        ps_pv = ps("ps_pv", [P, 2, KB, S])
        ps_any = ps("ps_any", [P, 2, KB, S])

        ident = sb("ident", [P, P])
        zeros = sb("zeros", [P, P])
        w_raw = sb("w_raw", [P, 4, KB, D])
        w_hi = sb("w_hi", [P, 4, KB, D], F32R)
        w_lo = sb("w_lo", [P, 4, KB, D], F32R)
        w1 = sb("w1", [P, KB, A])
        b1_col = sb("b1_col", [A, 1])
        v_col = sb("v_col", [A, 1])
        v_wide = sb("v_wide", [A, P])
        bqk_raw = sb("bqk_raw", [P, 2, 2])
        bqk_col = sb("bqk_col", [P, 3, 2])
        bin_col = sb("bin_col", [P, KB, 2])
        bv_wide = sb("bv_wide", [P, D])
        bo_wide = sb("bo_wide", [P, D])
        headsum = sb("headsum", [P, NJ])
        len_i = sb("len_i", [B, 1], I32)
        len_f = sb("len_f", [B, 1])
        key_pos = sb("key_pos", [B, S])
        mask_row = sb("mask_row", [B, S], F32)
        kind_i = sb("kind_i", [P, B], I32)
        kind_f = sb("kind_f", [P, B])
        is0 = sb("is0", [P, B])
        is1 = sb("is1", [P, B])
        code = sb("code", [P, B])
        rowpos = sb("rowpos", [P, KB])
        side_of = sb("side_of", [P, KB, S])
        cnt = sb("cnt", [P, B, KB])
        cnt_a = sb("cnt_a", [P, KB])
        cnt_b = sb("cnt_b", [P, KB])

        x_sb = sb("x_sb", [P, 2, KB, D])
        s_sb = sb("s_sb", [P, 2, KB, D])
        xt_hi = sb("xt_hi", [P, KB, S], F32R)
        xt_lo = sb("xt_lo", [P, KB, S], F32R)
        st_hi = sb("st_hi", [P, KB, S], F32R)
        st_lo = sb("st_lo", [P, KB, S], F32R)
        q_full = sb("q_full", [P, 2, S])
        k_full = sb("k_full", [P, 2, S])
        q_hi = sb("q_hi", [P, 2, S], F32R)
        q_lo = sb("q_lo", [P, 2, S], F32R)
        k_hi = sb("k_hi", [P, 2, S], F32R)
        k_lo = sb("k_lo", [P, 2, S], F32R)
        prod = sb("prod", [P, 2, S])
        q_rows = [sb(f"q_rows{i}", [P, NJ, S], F32R) for i in range(2)]
        k_rows = [sb(f"k_rows{i}", [P, NJ, S], F32R) for i in range(2)]
        v_aug = [sb(f"v_aug{i}", [P, KB, H, 32]) for i in range(2)]
        v_self = sb("v_self", [P, 2, KB, D])
        s_self = sb("s_self", [P, 2, KB, H])
        s_max = sb("s_max", [P, 2, KB, H])
        t_max = sb("t_max", [P, 2, KB, H])
        neg_max = sb("neg_max", [P, KB, NG, 2, 2, 2])
        mt_sb = sb("mt_sb", [8, 2, S], F32)
        p_arg = sb("p_arg", [P, KB, H])
        p_self = sb("p_self", [P, KB, H])
        pt = sb("pt", [P, 2 * GRP, KB, S])
        o_sb = sb("o_sb", [P, NG, S])
        vs_p = sb("vs_p", [P, KB, D])
        den = sb("den", [P, KB, H])
        rden = sb("rden", [P, KB, H])
        num = sb("num", [P, KB, D])
        attn = sb("attn", [P, KB, D])
        at_hi = sb("at_hi", [P, KB, S], F32R)
        at_lo = sb("at_lo", [P, KB, S], F32R)
        xr_sb = sb("xr_sb", [P, KB, D])
        x_bo = sb("x_bo", [P, KB, D])
        x1 = sb("x1", [P, KB, D])
        x1t = sb("x1t", [P, KB, S])
        z_sb = sb("z_sb", [A, S])
        hidden = sb("hidden", [P, KB, S])
        masked = sb("masked", [P, KB, S])
        row_max = sb("row_max", [P, KB])
        pool_p = sb("pool_p", [P, KB, S])
        pool_pt = sb("pool_pt", [P, KB, S])
        pool_sum = sb("pool_sum", [P, KB])
        pool_den = sb("pool_den", [P, KB])
        pool_r = sb("pool_r", [P, KB])
        o_out = sb("o_out", [P, KB, D])

        q_spill = nc.dram_tensor("q_spill", [2, 3, P, S], F32).ap()
        k_spill = nc.dram_tensor("k_spill", [2, 3, P, S], F32).ap()
        mask_dram = nc.dram_tensor("mask_dram", [B, S], F32).ap()

        consts_loaded = sem("consts_loaded")
        lens_loaded = sem("lens_loaded")
        weights_loaded = sem("weights_loaded")
        pool_zero = sem("pool_zero")
        pool_const = sem("pool_const")
        masks_ready = sem("masks_ready")
        masks_stored = sem("masks_stored")
        dve_const = sem("dve_const")
        w_hi_ready = sem("w_hi_ready")
        w_lo_ready = sem("w_lo_ready")
        w_scaled = sem("w_scaled")
        bias_ready = sem("bias_ready")
        bias_copied = sem("bias_copied")
        rows_one = sem("rows_one")
        x_loaded = [sem(f"x_loaded{i}") for i in range(2)]
        s_loaded = [sem(f"s_loaded{i}") for i in range(2)]
        xr_loaded = sem("xr_loaded")
        xt_ready, xt_hi_done, xt_lo_done = sem("xt_ready"), sem("xt_hi_done"), sem("xt_lo")
        st_ready, st_hi_done, st_lo_done = sem("st_ready"), sem("st_hi_done"), sem("st_lo")
        q_ready, q_full_done, q_copied, q_lo_done = sem("q_ready"), sem("q_full_done"), sem("q_copied"), sem("q_lo_done")
        k_ready, k_full_done, k_copied, k_lo_done = sem("k_ready"), sem("k_full_done"), sem("k_copied"), sem("k_lo_done")
        q_spilled, k_spilled = sem("q_spilled"), sem("k_spilled")
        q_placed, k_placed = sem("q_placed"), sem("k_placed")
        ks_ready, prod_done, ss_ready, ss_copied = sem("ks_ready"), sem("prod_done"), sem("ss_ready"), sem("ss_copied")
        v_ready, v_copied, vs_ready, vs_copied = sem("v_ready"), sem("v_copied"), sem("vs_ready"), sem("vs_copied")
        max_scored, max_found = sem("max_scored"), sem("max_found")
        total_max, neg_hi, neg_done = sem("total_max"), sem("neg_hi"), sem("neg_done")
        mt_ready, mt_copied = sem("mt_ready"), sem("mt_copied")
        max_placed = [sem(f"max_placed{g}") for g in range(NG)]
        p_arg_done, p_self_done = sem("p_arg_done"), sem("p_self_done")
        scored, p_ready, pv_ready, pv_copied = sem("scored"), sem("p_ready"), sem("pv_ready"), sem("pv_copied")
        vs_p_done, nat_ready = sem("vs_p_done"), sem("nat_ready")
        den_done, rden_done, num_done, attn_done = sem("den_done"), sem("rden_done"), sem("num_done"), sem("attn_done")
        at_ready, at_hi_done, at_lo_done = sem("at_ready"), sem("at_hi_done"), sem("at_lo")
        wo_ready, x_bo_done, x1_done = sem("wo_ready"), sem("x_bo_done"), sem("x1_done")
        x1t_ready, x1t_copied, z_ready, tanh_done = sem("x1t_ready"), sem("x1t_copied"), sem("z_ready"), sem("tanh_done")
        sb_ready, hidden_done, masked_done, row_max_done = sem("sb_ready"), sem("hidden_done"), sem("masked_done"), sem("row_max_done")
        pool_p_done, pt_ready, pt_copied = sem("pool_p_done"), sem("pt_ready"), sem("pt_copied")
        po_ready, pool_den_done, pool_r_done, out_done, out_stored = (
            sem("po_ready"), sem("pool_den_done"), sem("pool_r_done"), sem("out_done"), sem("out_stored"))

        def live(i, k):
            return not isinstance(i, int) or 0 <= 2 * i + k < B

        def count(i, k, per, done):
            n = i * (2 * per) + (k * per + done)
            return n if not isinstance(i, int) or n > 0 else None

        def row(dram, i, k):
            names = " ".join("abc"[:len(dram.shape) - 1])
            return dram.rearrange(f"(i k) {names} -> i k {names}", k=2)[i + k // 2, k % 2]

        def bank_free(step, i, k):
            at = next(n for n, entry in enumerate(SHARED) if entry[0] == step)
            parity = k % 2
            bank = (at + len(SHARED) * parity) % 2
            back = at
            for _ in range(2 * len(SHARED)):
                back -= 2
                name, offset, (reader, done) = SHARED[back % len(SHARED)]
                kk = k + back // len(SHARED) + offset
                if live(i, kk):
                    return bank, sems[reader], count(i, kk, PER_BATCH.get(reader, 1), done)
            return bank, None, None

        LOOP_FROM, LOOP_TO = 1, 3
        BEFORE = [(-1, 1), (0, 0), (0, 1)]
        AFTER = [(3, 0), (3, 1), (4, 0), (4, 1)]

        x_rows = x.rearrange("b (t p) d -> b p t d", p=P)
        s_rows = side.rearrange("b (t p) d -> b p t d", p=P)
        out_rows = out.rearrange("b (t p) d -> b p t d", p=P)

        block = ctx.enter_context(nc.Block())

        @block.sync
        def _(sp):
            def load(i, k):
                if live(i, k):
                    par = k % 2
                    if (n := count(i, k, 1, -1)) is not None:
                        sp.wait_ge(xt_ready, n)
                    sp.dma_start(x_sb[:, par], row(x_rows, i, k)).then_inc(x_loaded[par], 16)
                    if (n := count(i, k, 1, -1)) is not None:
                        sp.wait_ge(st_ready, n)
                    sp.dma_start(s_sb[:, par], row(s_rows, i, k)).then_inc(s_loaded[par], 16)

            def spill(i, k, hi, lo, lo_done, pattern, dram, placed, placed_per, spilled):
                n_lo = held(count(i, k, 1, 1))
                if (n := held(count(i, k, placed_per, 0))) is not None:
                    sp.wait_ge(placed, n)
                sp.wait_ge(lo_done, n_lo)
                for c, part in enumerate(pattern):
                    src = (hi, lo)[part][:].bitcast(F32)
                    sp.dma_start(dram[:, c].rearrange("e p t -> p e t"), src).then_inc(spilled, 16)

            def held(n):
                return n if n is None or isinstance(n, int) else sp.to_reg(n)

            def place(dram, spilled, n_spilled, rows, placed):
                sp.wait_ge(spilled, n_spilled)
                for e in range(2):
                    sp.dma_start(rows[64 * e:64 * e + ROWS].bitcast(F32),
                                 dram[e].rearrange("c (d j) t -> (c d) j t", d=DH)).then_inc(placed, 16)

            def place_max(i, k, g):
                par = k % 2
                sp.wait_ge(mt_copied, count(i, k, NG, g + 1))
                for e in range(2):
                    sp.dma_start(q_rows[par][64 * e + R_MAX:64 * e + R_MAX + 2, 2 * g:2 * g + 2, :].bitcast(F32),
                                 mt_sb[4 * e:4 * e + 4, g % 2, :]).then_inc(max_placed[g], 16)

            def period(i, k):
                b, nxt, prv, old = (i, k), (i, k + 1), (i, k - 1), (i, k - 2)
                if live(*prv):
                    place_max(*prv, 3)
                if live(*nxt):
                    spill(*nxt, q_hi, q_lo, q_lo_done, (0, 0, 1), q_spill, q_placed, 32, q_spilled)
                    spill(*nxt, k_hi, k_lo, k_lo_done, (0, 1, 0), k_spill, k_placed, 48, k_spilled)
                if live(*b):
                    place_max(*b, 0)
                if live(*prv):
                    if (n := count(*prv, 1, 0)) is not None:
                        sp.wait_ge(x_bo_done, n)
                    sp.dma_start(xr_sb[:], row(x_rows, *prv)).then_inc(xr_loaded, 16)
                if live(*nxt):
                    par = (k + 1) % 2
                    n_spilled = held(count(*nxt, 48, 48))
                    if (n := held(count(*nxt, H, -H))) is not None:
                        sp.wait_ge(scored, n)
                    else:
                        sp.wait_ge(rows_one, 1)
                    place(q_spill, q_spilled, n_spilled, q_rows[par], q_placed)
                    place(k_spill, k_spilled, n_spilled, k_rows[par], k_placed)
                    mask = row(mask_dram, *nxt).unsqueeze(0).unsqueeze(0).broadcast_to([2, NJ, S])
                    if isinstance(i, int):
                        sp.wait_ge(masks_stored, 16)
                    sp.dma_start(k_rows[par][R_MASK:R_MASK + 65:64].bitcast(F32), mask).then_inc(k_placed, 16)
                load(i, k + 2)
                if live(*b):
                    place_max(*b, 1)
                    place_max(*b, 2)

            sp.dma_start(x_sb[:, 0], x_rows[0]).then_inc(x_loaded[0], 16)
            sp.dma_start(s_sb[:, 0], s_rows[0]).then_inc(s_loaded[0], 16)
            for n, w in enumerate((Wq, Wk, Wv, Wo)):
                sp.dma_start(w_raw[:, n], w.rearrange("(k p) n -> p k n", p=P)).then_inc(weights_loaded, 16)
            sp.dma_start(len_i[:], seq_len.unsqueeze(1)).then_inc(lens_loaded, 16)
            sp.dma_start(kind_i[:], kind.partition_broadcast(P)).then_inc(lens_loaded, 16)
            with nc.allow_non_contiguous_dma("bias vectors, once"):
                for n, vec in enumerate((bq, bk)):
                    sp.dma_start(bqk_raw[:, n, :], vec.rearrange("(j e d) -> d j e", e=2, d=DH)
                                 ).then_inc(consts_loaded, 16)
                for n, vec in enumerate((b_self, b_prev)):
                    sp.dma_start(bin_col[:, :, n], vec.rearrange("a b (k p) -> p (a b k)", p=P)
                                 ).then_inc(consts_loaded, 16)
            sp.dma_start(bv_wide[:], bv.partition_broadcast(P)).then_inc(consts_loaded, 16)
            sp.dma_start(bo_wide[:], bo.partition_broadcast(P)).then_inc(consts_loaded, 16)
            sp.dma_start(w1[:], W1.rearrange("(k p) a -> p k a", p=P)).then_inc(consts_loaded, 16)
            sp.dma_start(b1_col[:], b1.unsqueeze(1)).then_inc(consts_loaded, 16)
            sp.dma_start(v_col[:], v.unsqueeze(1)).then_inc(consts_loaded, 16)
            sp.wait_ge(masks_ready, 1)
            sp.dma_start(mask_dram, mask_row[:]).then_inc(masks_stored, 16)

            for i, k in BEFORE:
                period(i, k)
            with sp.Fori(LOOP_FROM, LOOP_TO) as i:
                for k in range(2):
                    period(i, k)
            for i, k in AFTER:
                period(i, k)
            sp.wait_ge(out_stored, 16 * B)

        @block.gpsimd
        def _(pool):
            nc.gpsimd.memset(ident[:], 0.0).then_inc(pool_zero, 1)
            nc.gpsimd.memset(headsum[:], 0.0).then_inc(pool_zero, 1)
            nc.gpsimd.memset(side_of[:], 0.0).then_inc(pool_zero, 1)
            pool.wait_ge(pool_zero, 3)
            nc.gpsimd.affine_select(out=ident[:], in_=ident[:], compare_op=ALU.not_equal, fill=1.0, base=0,
                                    pattern=[[-1, P]], channel_multiplier=1).then_inc(pool_const, 1)
            nc.gpsimd.iota(key_pos[:], pattern=[[1, S]], base=0, channel_multiplier=0,
                           allow_small_or_imprecise_dtypes=True).then_inc(pool_const, 1)
            for d in range(DH):
                nc.gpsimd.affine_select(out=headsum[:], in_=headsum[:], compare_op=ALU.not_equal, fill=1.0,
                                        base=-NJ * d, pattern=[[-1, NJ]], channel_multiplier=1
                                        ).then_inc(pool_const, 1)
                pool.wait_ge(pool_const, 3 + d)
            nc.gpsimd.iota(rowpos[:], pattern=[[P, KB]], base=0, channel_multiplier=1,
                           allow_small_or_imprecise_dtypes=True).then_inc(pool_const, 1)
            nc.gpsimd.affine_select(out=side_of[:], in_=side_of[:], compare_op=ALU.is_ge, fill=1.0, base=0,
                                    pattern=[[P, KB], [-1, S]], channel_multiplier=1).then_inc(pool_const, 1)
            pool.wait_ge(pool_const, 4 + DH)
            nc.gpsimd.affine_select(out=side_of[:], in_=side_of[:], compare_op=ALU.is_ge, fill=-1.0, base=0,
                                    pattern=[[-P, KB], [1, S]], channel_multiplier=-1).then_inc(pool_const, 1)


            def split_lo(i, k, full_done, hi_done, full, hi, lo, lo_done, spilled):
                pool.wait_ge(full_done, count(i, k, 1, 1))
                pool.wait_ge(hi_done, count(i, k, 1, 1))
                if (n := count(i, k, 48, 0)) is not None:
                    pool.wait_ge(spilled, n)
                nc.gpsimd.tensor_tensor(lo[:], full[:], hi[:].bitcast(F32), ALU.subtract).then_inc(lo_done, 1)

            def period(i, k):
                b, nxt, prv, old = (i, k), (i, k + 1), (i, k - 1), (i, k - 2)
                if live(*nxt):
                    split_lo(*nxt, q_full_done, q_copied, q_full, q_hi, q_lo, q_lo_done, q_spilled)
                    split_lo(*nxt, k_full_done, k_copied, k_full, k_hi, k_lo, k_lo_done, k_spilled)
                if live(*prv):
                    par = (k - 1) % 2
                    pool.wait_ge(xr_loaded, count(*prv, 16, 16))
                    if (n := count(*prv, 1, 0)) is not None:
                        pool.wait_ge(x1_done, n)
                    nc.gpsimd.tensor_tensor(x_bo[:], xr_sb[:], bo_wide[:].unsqueeze(1).broadcast_to([P, KB, D]),
                                            ALU.add).then_inc(x_bo_done, 1)
                    pool.wait_ge(p_self_done, count(*prv, 1, 1))
                    pool.wait_ge(vs_copied, count(*prv, 1, 1))
                    if (n := count(*prv, 2, 0)) is not None:
                        pool.wait_ge(num_done, n)
                    for t in range(KB):
                        last = nc.gpsimd.tensor_tensor(
                            vs_p[:, t].rearrange("p (h d) -> p h d", d=DH),
                            v_self[:, par, t].rearrange("p (h d) -> p h d", d=DH),
                            p_self[:, t].unsqueeze(2).broadcast_to([P, H, DH]), ALU.mult)
                    last.then_inc(vs_p_done, 1)
                    if (n := count(*prv, 1, 0)) is not None:
                        pool.wait_ge(at_ready, n)
                    for t in range(KB):
                        pool.wait_ge(num_done, count(*prv, 2, t + 1))
                        nc.gpsimd.tensor_tensor(
                            attn[:, t].rearrange("p (h d) -> p h d", d=DH),
                            num[:, t].rearrange("p (h d) -> p h d", d=DH),
                            rden[:, t].unsqueeze(2).broadcast_to([P, H, DH]), ALU.mult).then_inc(attn_done, 1)

            for i, k in BEFORE:
                period(i, k)
            with pool.Fori(LOOP_FROM, LOOP_TO) as i:
                for k in range(2):
                    period(i, k)
            for i, k in AFTER:
                period(i, k)

        @block.scalar
        def _(act):
            def scalar_max_t(i, k, g):
                act.wait_ge(mt_ready, count(i, k, NG, g + 1))
                if g >= 2:
                    act.wait_ge(max_placed[g - 2], count(i, k, 32, 32))
                elif (n := count(i, k, 32, 0)) is not None:
                    act.wait_ge(max_placed[g + 2], n)
                bank = bank_free(f"MT{g}", i, k + (1 if g == 3 else 0))[0]
                nc.scalar.activation(mt_sb[:, g % 2, :], ps_any[0:8, bank, 0, :], ACT.Copy).then_inc(mt_copied, 1)

            def exps(i, k, h):
                act.wait_ge(scored, count(i, k, H, h + 1))
                if (n := count(i, k, NG, h // GRP - 1)) is not None:
                    act.wait_ge(pv_ready, n)
                nc.scalar.activation(pt[:, h % 8], ps_exp[:, h % 2], ACT.Exp).then_inc(p_ready, 1)

            def pv_copy(i, k, g):
                act.wait_ge(pv_ready, count(i, k, NG, g + 1))
                if (n := count(i, k, 2, 0)) is not None:
                    act.wait_ge(nat_ready, n)
                nc.scalar.activation(o_sb[:, g], ps_pv[:, g % 2, 0, :], ACT.Copy).then_inc(pv_copied, 1)

            def period(i, k):
                b, nxt, prv, old = (i, k), (i, k + 1), (i, k - 1), (i, k - 2)
                for s in range(SLOTS):
                    g = {1: 1, 5: 2, 9: 3, 13: 0}.get(s)
                    if g is not None and live(*(b if g == 0 else prv)):
                        pv_copy(*(b if g == 0 else prv), g)
                    h = (s - LAG) % SLOTS
                    if live(*(b if s >= LAG else prv)):
                        exps(*(b if s >= LAG else prv), h)
                    if s == 0 and live(*nxt):
                        act.wait_ge(xt_ready, count(*nxt, 1, 1))
                        if (n := count(*nxt, 1, 0)) is not None:
                            act.wait_ge(v_ready, n)
                        nc.scalar.activation(xt_hi[:], ps_any[:, bank_free("TX", i, k)[0]], ACT.Copy
                                             ).then_inc(xt_hi_done, 1)
                        act.wait_ge(st_ready, count(*nxt, 1, 1))
                        if (n := count(*nxt, 1, 0)) is not None:
                            act.wait_ge(vs_ready, n)
                        nc.scalar.activation(st_hi[:], ps_any[:, bank_free("TS", i, k)[0]], ACT.Copy
                                             ).then_inc(st_hi_done, 1)
                    if s == 1:
                        if live(*old):
                            act.wait_ge(z_ready, count(*old, 1, 1))
                            if (n := count(*old, 1, 0)) is not None:
                                act.wait_ge(sb_ready, n)
                            nc.scalar.activation(z_sb[:], ps_any[0:A, bank_free("Z", i, k)[0], 0, :], ACT.Tanh,
                                                 bias=b1_col[:, 0:1]).then_inc(tanh_done, 1)
                        if live(*prv):
                            scalar_max_t(*prv, 3)
                            act.wait_ge(p_arg_done, count(*prv, 1, 1))
                            if (n := count(*prv, 1, 0)) is not None:
                                act.wait_ge(vs_p_done, n)
                                act.wait_ge(den_done, count(*prv, 2, 0))
                            nc.scalar.activation(p_self[:], p_arg[:], ACT.Exp).then_inc(p_self_done, 1)
                        if live(*nxt):
                            qk_copy(*nxt, "Q", i, k)
                    if s == 2 and live(*nxt):
                        qk_copy(*nxt, "K", i, k)
                    if s == 4 and live(*old):
                        act.wait_ge(row_max_done, count(*old, 1, 1))
                        if (n := count(*old, 1, 0)) is not None:
                            act.wait_ge(pt_ready, n)
                            act.wait_ge(pool_den_done, n)
                        for t in range(KB):
                            last = nc.scalar.activation(pool_p[:, t], masked[:, t], ACT.Exp,
                                                        bias=row_max[:, t:t + 1], accum_out=pool_sum[:, t:t + 1])
                            last.then_inc(pool_p_done, 1)
                    if s == 5:
                        if live(*b):
                            scalar_max_t(*b, 0)
                        if live(*nxt):
                            par = (k + 1) % 2
                            act.wait_ge(ss_ready, count(*nxt, 1, 1))
                            if (n := count(*nxt, 1, -1)) is not None:
                                act.wait_ge(p_arg_done, n)
                            nc.scalar.activation(
                                s_self[:, par].rearrange("p t (j e) -> p t j e", e=2),
                                ps_any[:, bank_free("SS", i, k)[0], 0, 0:2 * H].rearrange(
                                    "p (t e j) -> p t j e", t=KB, e=2), ACT.Copy).then_inc(ss_copied, 1)
                    if s == 7 and live(*old):
                        act.wait_ge(pt_ready, count(*old, 1, 1))
                        if (n := count(*old, 1, 0)) is not None:
                            act.wait_ge(po_ready, n)
                        nc.scalar.activation(pool_pt[:], ps_any[:, bank_free("PT", i, k)[0]], ACT.Copy
                                             ).then_inc(pt_copied, 1)
                    if s == 9 and live(*b):
                        scalar_max_t(*b, 1)
                    if s == 10 and live(*old):
                        act.wait_ge(out_done, count(*old, 1, 1))
                        act.dma_start(row(out_rows, *old), o_out[:]).then_inc(out_stored, 16)
                    if s == 12 and live(*prv):
                        act.wait_ge(at_ready, count(*prv, 1, 1))
                        if (n := count(*prv, 1, 0)) is not None:
                            act.wait_ge(wo_ready, n)
                        nc.scalar.activation(at_hi[:], ps_any[:, bank_free("AT", i, k)[0]], ACT.Copy
                                             ).then_inc(at_hi_done, 1)
                    if s == 13 and live(*b):
                        scalar_max_t(*b, 2)
                    if s == 15 and live(*prv):
                        act.wait_ge(x1t_ready, count(*prv, 1, 1))
                        if (n := count(*prv, 1, 0)) is not None:
                            act.wait_ge(z_ready, n)
                        nc.scalar.activation(x1t[:], ps_any[:, bank_free("X1T", i, k)[0]], ACT.Copy
                                             ).then_inc(x1t_copied, 1)

            def qk_copy(i, k, step, pi, pk):
                ready, full, hi, full_done, hi_done, lo_done, spilled, n_bias = {
                    "Q": (q_ready, q_full, q_hi, q_full_done, q_copied, q_lo_done, q_spilled, 0),
                    "K": (k_ready, k_full, k_hi, k_full_done, k_copied, k_lo_done, k_spilled, 1)}[step]
                bank = bank_free(step, pi, pk)[0]
                act.wait_ge(ready, count(i, k, 1, 1))
                if (n := count(i, k, 1, 0)) is not None:
                    act.wait_ge(lo_done, n)
                    if step == "Q":
                        act.wait_ge(prod_done, n)
                else:
                    act.wait_ge(bias_copied, 1)
                for m in range(2):
                    last = nc.scalar.activation(full[:, m], ps_any[:, bank, m], ACT.Identity,
                                                bias=bqk_col[:, n_bias, m:m + 1])
                last.then_inc(full_done, 1)
                if (n := count(i, k, 48, 0)) is not None:
                    act.wait_ge(spilled, n)
                for m in range(2):
                    last = nc.scalar.activation(hi[:, m], ps_any[:, bank, m], ACT.Identity,
                                                bias=bqk_col[:, n_bias, m:m + 1])
                last.then_inc(hi_done, 1)

            for i, k in BEFORE:
                period(i, k)
            with act.Fori(LOOP_FROM, LOOP_TO) as i:
                for k in range(2):
                    period(i, k)
            for i, k in AFTER:
                period(i, k)

        @block.vector
        def _(dve):
            dve.wait_ge(weights_loaded, 64)
            nc.vector.tensor_scalar(w_raw[:, 0], w_raw[:, 0], QSCALE, None, ALU.mult).then_inc(w_scaled, 1)
            dve.wait_ge(w_scaled, 1)

            def permuted(w, n, k):
                return w[:, n, k].rearrange("p (e d j) -> p e d j", e=2, d=DH)

            for n in range(4):
                for kb in range(KB):
                    if n < 2:
                        for e in range(2):
                            src = w_raw[:, n, kb].rearrange("p (j e d) -> p e d j", e=2, d=DH)[:, e]
                            nc.vector.tensor_copy(permuted(w_hi, n, kb)[:, e], src).then_inc(w_hi_ready, 1)
                    else:
                        nc.vector.tensor_copy(w_hi[:, n, kb], w_raw[:, n, kb]).then_inc(w_hi_ready, 1)
            dve.wait_ge(w_hi_ready, 12)
            for n in range(4):
                for kb in range(KB):
                    if n < 2:
                        for e in range(2):
                            src = w_raw[:, n, kb].rearrange("p (j e d) -> p e d j", e=2, d=DH)[:, e]
                            nc.vector.tensor_tensor(permuted(w_lo, n, kb)[:, e], src,
                                                    permuted(w_hi, n, kb)[:, e].bitcast(F32),
                                                    ALU.subtract).then_inc(w_lo_ready, 1)
                    else:
                        nc.vector.tensor_tensor(w_lo[:, n, kb], w_raw[:, n, kb], w_hi[:, n, kb].bitcast(F32),
                                                ALU.subtract).then_inc(w_lo_ready, 1)
            for par in range(2):
                nc.vector.memset(q_rows[par][:].bitcast(F32), 1.0)
                nc.vector.memset(k_rows[par][:].bitcast(F32), 1.0)
                nc.vector.memset(v_aug[par][:], 0.0)
            nc.vector.memset(zeros[:], 0.0).then_inc(rows_one, 1)
            dve.wait_ge(lens_loaded, 32)
            dve.wait_ge(rows_one, 1)
            dve.wait_ge(consts_loaded, 9 * 16)
            for par in range(2):
                nc.vector.memset(v_aug[par][:, :, :, DH:DH + 1], 1.0)
            nc.vector.tensor_copy(len_f[:], len_i[:]).then_inc(dve_const, 1)
            nc.vector.tensor_copy(kind_f[:], kind_i[:]).then_inc(dve_const, 1)
            nc.vector.tensor_scalar(v_wide[:], zeros[0:A, :], v_col[:, 0:1], None, ALU.add).then_inc(dve_const, 1)
            dve.wait_ge(dve_const, 3)
            dve.wait_ge(pool_const, 5 + DH)
            nc.vector.tensor_scalar(mask_row[:], key_pos[:], len_f[:, 0:1], MASKED, ALU.is_ge, ALU.mult
                                    ).then_inc(masks_ready, 1)
            nc.vector.tensor_scalar(is0[:], kind_f[:], 0.0, None, ALU.is_equal).then_inc(dve_const, 1)
            nc.vector.tensor_scalar(is1[:], kind_f[:], 1.0, None, ALU.is_equal).then_inc(dve_const, 1)
            dve.wait_ge(dve_const, 5)
            nc.vector.tensor_tensor(code[:], is0[:], is1[:], ALU.subtract).then_inc(dve_const, 1)
            nc.vector.tensor_scalar(cnt_a[:], rowpos[:], float(2 - S), None, ALU.add).then_inc(dve_const, 1)
            nc.vector.tensor_scalar(cnt_b[:], rowpos[:], -1.0, 1.0, ALU.mult, ALU.add).then_inc(dve_const, 1)
            nc.vector.memset(cnt[:], float(S - 1)).then_inc(dve_const, 1)
            n_const = 9
            dve.wait_ge(dve_const, n_const)
            for sel, diff in ((is0, cnt_a), (is1, cnt_b)):
                for t in range(KB):
                    nc.vector.scalar_tensor_tensor(out=cnt[:, :, t], in0=sel[:], scalar=diff[:, t:t + 1],
                                                   in1=cnt[:, :, t], op0=ALU.mult, op1=ALU.add
                                                   ).then_inc(dve_const, 1)
                n_const += KB
                dve.wait_ge(dve_const, n_const)
            nc.vector.tensor_scalar(bqk_raw[:, 0], bqk_raw[:, 0], QSCALE, None, ALU.mult).then_inc(dve_const, 1)
            dve.wait_ge(dve_const, n_const + 1)
            dve.wait_ge(bias_ready, 1)
            for n, b_of in enumerate((0, 1, 1)):
                last = nc.vector.tensor_tensor(bqk_col[:, n], ps_any[:, 1, 1, 2 * n:2 * n + 2], bqk_raw[:, b_of],
                                               ALU.add)
            last.then_inc(bias_copied, 1)

            def max_of(i, k, h):
                dve.wait_ge(max_scored, count(i, k, H, h + 1))
                nc.vector.tensor_reduce(s_max[:, k % 2, :, h], ps_max[:, h % 2], AX.X, ALU.max
                                        ).then_inc(max_found, 1)

            def group_max(i, k, g):
                par = k % 2
                heads = slice(GRP * g, GRP * g + GRP)
                dve.wait_ge(max_found, count(i, k, H, GRP * (g + 1)))
                dve.wait_ge(ss_copied, count(i, k, 1, 1))
                nc.vector.tensor_tensor(t_max[:, par, :, heads], s_max[:, par, :, heads],
                                        s_self[:, par, :, heads], ALU.max).then_inc(total_max, 1)
                dve.wait_ge(total_max, count(i, k, NG, g + 1))
                if (n := count(i, k, NG, g + 1 - NG)) is not None:
                    dve.wait_ge(mt_ready, n)
                for t in range(KB):
                    top = t_max[:, par, t, heads].rearrange("p (j e) -> p e j", e=2)
                    last = nc.vector.tensor_scalar(neg_max[:, t, g, :, 0].bitcast(F32R), top, -1.0, None, ALU.mult)
                last.then_inc(neg_hi, 1)
                dve.wait_ge(neg_hi, count(i, k, NG, g + 1))
                for t in range(KB):
                    top = t_max[:, par, t, heads].rearrange("p (j e) -> p e j", e=2)
                    last = nc.vector.scalar_tensor_tensor(out=neg_max[:, t, g, :, 1].bitcast(F32R), in0=top,
                                                          scalar=-1.0, in1=neg_max[:, t, g, :, 0],
                                                          op0=ALU.mult, op1=ALU.subtract)
                last.then_inc(neg_done, 1)

            def period(i, k):
                b, nxt, prv, old = (i, k), (i, k + 1), (i, k - 1), (i, k - 2)
                for s in range(SLOTS):
                    if s == 0 and live(*prv):
                        group_max(*prv, 3)
                        if (n := count(*prv, 1, 0)) is not None:
                            dve.wait_ge(p_self_done, n)
                        par = (k - 1) % 2
                        nc.vector.tensor_tensor(p_arg[:], s_self[:, par], t_max[:, par], ALU.subtract
                                                ).then_inc(p_arg_done, 1)
                    if s in (4, 8, 12) and live(*b):
                        group_max(*b, s // 4 - 1)
                    if live(*b):
                        max_of(*b, s)
                    if s == 0 and live(*nxt):
                        dve.wait_ge(xt_hi_done, count(*nxt, 1, 1))
                        nc.vector.tensor_tensor(xt_lo[:], ps_any[:, bank_free("TX", i, k)[0]],
                                                xt_hi[:].bitcast(F32), ALU.subtract).then_inc(xt_lo_done, 1)
                        dve.wait_ge(st_hi_done, count(*nxt, 1, 1))
                        nc.vector.tensor_tensor(st_lo[:], ps_any[:, bank_free("TS", i, k)[0]],
                                                st_hi[:].bitcast(F32), ALU.subtract).then_inc(st_lo_done, 1)
                    if s == 3 and live(*old):
                        kk = k - 2
                        codes = code[:].rearrange("p (i k) -> p i k", k=2)
                        if (n := count(*old, 1, 0)) is not None:
                            dve.wait_ge(masked_done, n)
                        nc.vector.tensor_scalar(hidden[:], side_of[:], codes[:, i + kk // 2, kk % 2:kk % 2 + 1],
                                                MASKED, ALU.is_equal, ALU.mult).then_inc(hidden_done, 1)
                    if s == 4 and live(*old):
                        dve.wait_ge(sb_ready, count(*old, 1, 1))
                        dve.wait_ge(hidden_done, count(*old, 1, 1))
                        if (n := count(*old, 2, 0)) is not None:
                            dve.wait_ge(pool_p_done, n)
                        nc.vector.tensor_tensor(
                            masked[:], hidden[:],
                            ps_any[:, bank_free("SB", i, k)[0], 0].unsqueeze(1).broadcast_to([P, KB, S]),
                            ALU.add).then_inc(masked_done, 1)
                        dve.wait_ge(masked_done, count(*old, 1, 1))
                        nc.vector.tensor_reduce(row_max[:], masked[:], AX.X, ALU.max, negate=True
                                                ).then_inc(row_max_done, 1)
                    if s == 4 and live(*nxt):
                        dve.wait_ge(ks_ready, count(*nxt, 1, 1))
                        dve.wait_ge(q_full_done, count(*nxt, 1, 1))
                        if (n := count(*nxt, 1, 0)) is not None:
                            dve.wait_ge(ss_ready, n)
                        for m in range(2):
                            last = nc.vector.scalar_tensor_tensor(
                                out=prod[:, m], in0=ps_any[:, bank_free("KS", i, k)[0], m],
                                scalar=bqk_col[:, 2, m:m + 1], in1=q_full[:, m], op0=ALU.add, op1=ALU.mult)
                        last.then_inc(prod_done, 1)
                    if s == 9 and live(*old):
                        dve.wait_ge(pool_p_done, count(*old, 2, 2))
                        kk = k - 2
                        rows_cnt = cnt[:].rearrange("p (i k) t -> p i k t", k=2)[:, i + kk // 2, kk % 2]
                        nc.vector.tensor_tensor(pool_den[:], pool_sum[:], rows_cnt, ALU.mult
                                                ).then_inc(pool_den_done, 1)
                        dve.wait_ge(pool_den_done, count(*old, 1, 1))
                        nc.vector.reciprocal(pool_r[:], pool_den[:]).then_inc(pool_r_done, 1)
                        dve.wait_ge(pool_r_done, count(*old, 1, 1))
                        dve.wait_ge(po_ready, count(*old, 1, 1))
                        if (n := count(*old, 16, 0)) is not None:
                            dve.wait_ge(out_stored, n)
                        for t in range(KB):
                            last = nc.vector.scalar_tensor_tensor(
                                out=o_out[:, t], in0=ps_any[:, bank_free("PO", i, k)[0], t],
                                scalar=pool_r[:, t:t + 1], in1=x1[:, t], op0=ALU.mult, op1=ALU.add)
                        last.then_inc(out_done, 1)
                    if s == 9 and live(*nxt):
                        dve.wait_ge(v_ready, count(*nxt, 1, 1))
                        if (n := count(*nxt, NG, -NG)) is not None:
                            dve.wait_ge(pv_ready, n)
                        for t in range(KB):
                            last = nc.vector.tensor_tensor(
                                v_aug[(k + 1) % 2][:, t, :, 0:DH],
                                ps_any[:, bank_free("V", i, k)[0], t].rearrange("p (h d) -> p h d", d=DH),
                                bv_wide[:].rearrange("p (h d) -> p h d", d=DH), ALU.add)
                        last.then_inc(v_copied, 1)
                    if s == 11 and live(*prv):
                        for t in range(KB):
                            bank = ps_any[:, bank_free(f"NAT{t}", i, k)[0]].rearrange(
                                "p t (h c) -> p (t h) c", c=32)
                            dve.wait_ge(nat_ready, count(*prv, 2, t + 1))
                            dve.wait_ge(p_self_done, count(*prv, 1, 1))
                            if (n := count(*prv, 2, t - 1)) is not None:
                                dve.wait_ge(attn_done, n)
                            nc.vector.tensor_tensor(den[:, t], bank[:, :, DH], p_self[:, t], ALU.add
                                                    ).then_inc(den_done, 1)
                            dve.wait_ge(den_done, count(*prv, 2, t + 1))
                            nc.vector.reciprocal(rden[:, t], den[:, t]).then_inc(rden_done, 1)
                            dve.wait_ge(vs_p_done, count(*prv, 1, 1))
                            dve.wait_ge(rden_done, count(*prv, 2, t + 1))
                            nc.vector.tensor_tensor(
                                num[:, t].rearrange("p (h d) -> p h d", d=DH), bank[:, :, 0:DH],
                                vs_p[:, t].rearrange("p (h d) -> p h d", d=DH), ALU.add).then_inc(num_done, 1)
                    if s == 12 and live(*nxt):
                        dve.wait_ge(vs_ready, count(*nxt, 1, 1))
                        if (n := count(*nxt, 1, -1)) is not None:
                            dve.wait_ge(vs_p_done, n)
                        nc.vector.tensor_tensor(v_self[:, (k + 1) % 2], ps_any[:, bank_free("VS", i, k)[0]],
                                                bv_wide[:].unsqueeze(1).broadcast_to([P, KB, D]), ALU.add
                                                ).then_inc(vs_copied, 1)
                    if s == 12 and live(*prv):
                        dve.wait_ge(at_hi_done, count(*prv, 1, 1))
                        nc.vector.tensor_tensor(at_lo[:], ps_any[:, bank_free("AT", i, k)[0]],
                                                at_hi[:].bitcast(F32), ALU.subtract).then_inc(at_lo_done, 1)
                    if s == 14 and live(*prv):
                        dve.wait_ge(wo_ready, count(*prv, 1, 1))
                        dve.wait_ge(x_bo_done, count(*prv, 1, 1))
                        if (n := count(*prv, 1, 0)) is not None:
                            dve.wait_ge(out_done, n)
                        nc.vector.tensor_tensor(x1[:], ps_any[:, bank_free("WO", i, k)[0]], x_bo[:], ALU.add
                                                ).then_inc(x1_done, 1)

            for i, k in BEFORE:
                period(i, k)
            with dve.Fori(LOOP_FROM, LOOP_TO) as i:
                for k in range(2):
                    period(i, k)
            for i, k in AFTER:
                period(i, k)

        @block.tensor
        def _(pe):
            def products(out_of, hi, lo, w, n, stationary_w):
                for m in range(2):
                    terms = [(kb, a, c) for kb in range(KB) for a, c in ((0, 0), (0, 1), (1, 0))]
                    for j, (kb, a, c) in enumerate(terms):
                        act_part, w_part = (hi, lo)[a], (w_hi, w_lo)[c]
                        if stationary_w:
                            lhs, rhs = w_part[:, n, kb, P * m:P * m + P], act_part[:, kb, :]
                        else:
                            lhs, rhs = act_part[:, kb, P * m:P * m + P], w_part[:, n, kb, :]
                        last = pe.matmul(out_of[:, m], lhs, rhs, start=(j == 0), stop=(j == len(terms) - 1))
                return last

            def transposed(out_of, src):
                for kb in range(KB):
                    for t in range(KB):
                        last = pe.transpose(out_of[:, kb, P * t:P * t + P], src[:, t, P * kb:P * kb + P], ident[:])
                return last

            def take_bank(step, i, k):
                bank, reader, n = bank_free(step, i, k)
                if n is not None:
                    pe.wait_ge(reader, n)
                return ps_any[:, bank]

            def score_for_max(i, k, h):
                par, e, j = k % 2, h % 2, h // 2
                if h == 0:
                    pe.wait_ge(q_placed, count(i, k, 32, 32))
                    pe.wait_ge(k_placed, count(i, k, 48, 48))
                if (n := count(i, k, H, h - 1)) is not None:
                    pe.wait_ge(max_found, n)
                rows = slice(64 * e, 64 * e + KM)
                for t in range(KB):
                    last = pe.matmul(ps_max[:, e, t], q_rows[par][rows, j, P * t:P * t + P],
                                     k_rows[par][rows, j, :], start=True, stop=True)
                last.then_inc(max_scored, 1)

            def score_for_exp(i, k, h):
                par, e, j = k % 2, h % 2, h // 2
                if h % GRP == 0:
                    pe.wait_ge(max_placed[h // GRP], count(i, k, 32, 32))
                if (n := count(i, k, H, h - 1)) is not None:
                    pe.wait_ge(p_ready, n)
                rows = slice(64 * e, 64 * e + KF)
                for t in range(KB):
                    last = pe.matmul(ps_exp[:, e, t], k_rows[par][rows, j, P * t:P * t + P],
                                     q_rows[par][rows, j, :], start=True, stop=True)
                last.then_inc(scored, 1)

            def pv(i, k, g):
                par = k % 2
                pe.wait_ge(p_ready, count(i, k, H, GRP * (g + 1)))
                if g == 0:
                    pe.wait_ge(v_copied, count(i, k, 1, 1))
                if (n := count(i, k, NG, g - 1)) is not None:
                    pe.wait_ge(pv_copied, n)
                for t in range(KB):
                    for c in range(GRP):
                        h = GRP * g + c
                        last = pe.matmul(ps_pv[32 * c:32 * c + 32, g % 2, 0, :], v_aug[par][:, t, h, :],
                                         pt[:, h % 8, t, :], start=(t == 0), stop=(t == KB - 1),
                                         skip_group_check=True)
                last.then_inc(pv_ready, 1)

            def max_to_rows(i, k, g, pi, pk):
                bank = take_bank(f"MT{g}", pi, pk)
                pe.wait_ge(neg_done, count(i, k, NG, g + 1))
                for t in range(KB):
                    last = pe.transpose(bank[0:8, 0, P * t:P * t + P],
                                        neg_max[:, t, g].rearrange("p e c j -> p (e c j)"), ident[:])
                last.then_inc(mt_ready, 1)

            def period(i, k):
                b, nxt, prv, old = (i, k), (i, k + 1), (i, k - 1), (i, k - 2)
                for s in range(SLOTS):
                    if live(*b):
                        score_for_max(*b, s)
                    who = b if s >= LAG else prv
                    if live(*who):
                        score_for_exp(*who, (s - LAG) % SLOTS)
                    g = {12: 0, 0: 1, 4: 2, 8: 3}.get(s)
                    who = b if g == 0 else prv
                    if g is not None and live(*who):
                        pv(*who, g)
                    if s == 0 and live(*nxt):
                        par = (k + 1) % 2
                        bank = take_bank("TX", i, k)
                        pe.wait_ge(x_loaded[par], count(i + (k + 1) // 2, 0, 8, 16))
                        transposed(bank, x_sb[:, par]).then_inc(xt_ready, 1)
                        bank = take_bank("TS", i, k)
                        pe.wait_ge(s_loaded[par], count(i + (k + 1) // 2, 0, 8, 16))
                        transposed(bank, s_sb[:, par]).then_inc(st_ready, 1)
                    if s == 1:
                        if live(*old):
                            bank = take_bank("Z", i, k)
                            pe.wait_ge(x1t_copied, count(*old, 1, 1))
                            for kb in range(KB):
                                last = pe.matmul(bank[0:A, 0], w1[:, kb, :], x1t[:, kb, :],
                                                 start=(kb == 0), stop=(kb == KB - 1))
                            last.then_inc(z_ready, 1)
                        if live(*prv):
                            max_to_rows(*prv, 3, i, k)
                        if live(*nxt):
                            bank = take_bank("Q", i, k)
                            pe.wait_ge(st_hi_done, count(*nxt, 1, 1))
                            pe.wait_ge(st_lo_done, count(*nxt, 1, 1))
                            products(bank, st_hi, st_lo, "q", 0, True).then_inc(q_ready, 1)
                    if s == 2 and live(*nxt):
                        bank = take_bank("K", i, k)
                        pe.wait_ge(xt_hi_done, count(*nxt, 1, 1))
                        pe.wait_ge(xt_lo_done, count(*nxt, 1, 1))
                        products(bank, xt_hi, xt_lo, "k", 1, True).then_inc(k_ready, 1)
                    if s == 3:
                        if live(*old):
                            bank = take_bank("SB", i, k)
                            pe.wait_ge(tanh_done, count(*old, 1, 1))
                            pe.matmul(bank[:, 0], v_wide[:], z_sb[:], start=True, stop=True).then_inc(sb_ready, 1)
                        if live(*nxt):
                            bank = take_bank("KS", i, k)
                            products(bank, st_hi, st_lo, "k", 1, True).then_inc(ks_ready, 1)
                    if s == 5:
                        if live(*b):
                            max_to_rows(*b, 0, i, k)
                        if live(*nxt):
                            bank = take_bank("SS", i, k)
                            pe.wait_ge(prod_done, count(*nxt, 1, 1))
                            for t in range(KB):
                                for e in range(2):
                                    at = NJ * (2 * t + e)
                                    last = pe.matmul(bank[:, 0, at:at + NJ], prod[:, e, P * t:P * t + P],
                                                     headsum[:], start=True, stop=True)
                            last.then_inc(ss_ready, 1)
                    if s == 6 and live(*old):
                        bank = take_bank("PT", i, k)
                        pe.wait_ge(pool_p_done, count(*old, 2, 2))
                        transposed(bank, pool_p).then_inc(pt_ready, 1)
                    if s == 8 and live(*old):
                        bank = take_bank("PO", i, k)
                        pe.wait_ge(pt_copied, count(*old, 1, 1))
                        for t in range(KB):
                            for kb in range(KB):
                                last = pe.matmul(bank[:, t], pool_pt[:, kb, P * t:P * t + P], x1[:, kb, :],
                                                 start=(kb == 0), stop=(kb == KB - 1))
                        last.then_inc(po_ready, 1)
                    if s == 9:
                        if live(*b):
                            max_to_rows(*b, 1, i, k)
                        if live(*nxt):
                            bank = take_bank("V", i, k)
                            products(bank, xt_hi, xt_lo, "v", 2, False).then_inc(v_ready, 1)
                    if s == 10 and live(*prv):
                        for t in range(KB):
                            bank = take_bank(f"NAT{t}", i, k)
                            pe.wait_ge(pv_copied, count(*prv, NG, NG))
                            for gg in range(NG):
                                last = pe.transpose(bank[:, gg // 2, P * (gg % 2):P * (gg % 2) + P],
                                                    o_sb[:, gg, P * t:P * t + P], ident[:])
                            last.then_inc(nat_ready, 1)
                    if s == 11 and live(*nxt):
                        bank = take_bank("VS", i, k)
                        products(bank, st_hi, st_lo, "v", 2, False).then_inc(vs_ready, 1)
                    if s == 12 and live(*prv):
                        bank = take_bank("AT", i, k)
                        pe.wait_ge(attn_done, count(*prv, 2, 2))
                        transposed(bank, attn).then_inc(at_ready, 1)
                    if s == 13:
                        if live(*b):
                            max_to_rows(*b, 2, i, k)
                        if live(*prv):
                            bank = take_bank("WO", i, k)
                            pe.wait_ge(at_hi_done, count(*prv, 1, 1))
                            pe.wait_ge(at_lo_done, count(*prv, 1, 1))
                            products(bank, at_hi, at_lo, "o", 3, False).then_inc(wo_ready, 1)
                    if s == 15 and live(*prv):
                        bank = take_bank("X1T", i, k)
                        pe.wait_ge(x1_done, count(*prv, 1, 1))
                        transposed(bank, x1).then_inc(x1t_ready, 1)

            pe.wait_ge(w_lo_ready, 12)
            pe.wait_ge(consts_loaded, 9 * 16)
            for n, (w_of, b_of) in enumerate(((0, 0), (1, 1), (1, 0))):
                for m in range(2):
                    terms = [(part, kb) for part in (w_hi, w_lo) for kb in range(KB)]
                    for j, (part, kb) in enumerate(terms):
                        last = pe.matmul(ps_any[:, 1, 1, 2 * n + m:2 * n + m + 1],
                                         part[:, w_of, kb, P * m:P * m + P].bitcast(F32),
                                         bin_col[:, kb, b_of:b_of + 1], start=(j == 0), stop=(j == 3))
            last.then_inc(bias_ready, 1)
            pe.wait_ge(pool_const, 3 + DH)
            pe.wait_ge(bias_copied, 1)

            for i, k in BEFORE:
                period(i, k)
            with pe.Fori(LOOP_FROM, LOOP_TO) as i:
                for k in range(2):
                    period(i, k)
            for i, k in AFTER:
                period(i, k)


_INS = ["x", "fside_BxSxS_0", "itok_B_18_1004", "itok_B_0_2", "L0_cond_Wq", "L0_cond_bq", "L0_cond_Wk",
        "L0_cond_bk", "L0_cond_Wv", "L0_cond_bv", "L0_cond_Wo", "L0_cond_bo", "L0_cond_b_prev",
        "L0_cond_b_self", "L1_cond_W1", "L1_cond_b1", "L1_cond_v"]


def kernel(**inputs):
    import numpy as _np
    import concourse.bacc as _bacc
    from concourse.bass_utils import run_bass_kernel_spmd as _run

    nc = _bacc.Bacc("TRN2", target_bir_lowering=False, num_devices=1)
    arrays, args = {}, []
    for name in _INS:
        a = _np.ascontiguousarray(inputs[name])
        arrays[f"in_{name}"] = a
        args.append(nc.dram_tensor(f"in_{name}", a.shape, mybir.dt.from_np(a.dtype), kind="ExternalInput").ap())
    out = nc.dram_tensor("out_0", inputs["x"].shape, F32, kind="ExternalOutput").ap()
    build(nc, *args, out)
    return _run(nc, [arrays], core_ids=[0]).results[0]["out_0"]
```

```python
from contextlib import ExitStack

import concourse.bass as bass
from concourse import mybir

F32 = mybir.dt.float32
F32R = mybir.dt.float32r
I32 = mybir.dt.int32
ALU = mybir.AluOpType
ACT = mybir.ActivationFunctionType
AX = mybir.AxisListType

P = 128
MASKED = -1e30

SHARED = [
    ("TS", 1, ("st_lo", 1)), ("MT3", -1, ("mt_copied", 4)),
    ("WO", -2, ("x1_done", 1)),
    ("TX", 1, ("xt_lo", 1)),
    ("Q", 1, ("q_copied", 1)),
    ("X1T", -2, ("x1t_copied", 1)),
    ("MT0", 0, ("mt_copied", 1)), ("K", 1, ("k_copied", 1)),
    ("Z", -2, ("tanh_done", 1)),
    ("KS", 1, ("prod_done", 1)),
    ("SB", -2, ("masked_done", 1)),
    ("MT1", 0, ("mt_copied", 2)), ("V", 1, ("v_copied", 1)),
    ("NAT0", -1, ("num_done", 1)), ("NAT1", -1, ("num_done", 2)),
    ("PT", -2, ("pt_copied", 1)), ("SS", 1, ("ss_copied", 1)),
    ("MT2", 0, ("mt_copied", 3)), ("PO", -2, ("out_done", 1)),
    ("AT", -1, ("at_lo", 1)),
    ("VS", 1, ("vs_copied", 1)),
]
BANKS = 3
PER_BATCH = {"mt_copied": 4, "num_done": 2}


def build(nc, x, side, seq_len, kind, Wq, bq, Wk, bk, Wv, bv, Wo, bo, b_prev, b_self, W1, b1, v, out):
    B, S, D = x.shape
    DH = 16
    H = D // DH
    NJ = H // 2
    KB = D // P
    A = W1.shape[1]
    ROWS = 3 * DH
    R_MASK, R_MAX = ROWS, ROWS + 1
    KM = ROWS + 1
    KF = ROWS + 3
    SLOTS = H
    LAG = 8
    GRP = 4
    NG = H // GRP
    QSCALE = 1.0 / DH ** 0.5
    assert (S, D, H, KB, SLOTS) == (256, 256, 16, 2, 16)

    with ExitStack() as ctx:
        def sb(name, shape, dt=F32):
            return ctx.enter_context(nc.sbuf_tensor(name, shape, dt))

        def ps(name, shape):
            return ctx.enter_context(nc.psum_tensor(name, shape, F32))

        sems = {}
        assert len(SHARED) % BANKS == 0

        def sem(name):
            sems[name] = ctx.enter_context(nc.semaphore(name))
            return sems[name]

        ps_max = ps("ps_max", [P, 2, KB, S])
        ps_exp = ps("ps_exp", [P, 2, KB, S])
        ps_pv = ps("ps_pv", [P, KB, S])
        ps_any = ps("ps_any", [P, BANKS, KB, S])

        ident = sb("ident", [P, P])
        zeros = sb("zeros", [P, P])
        w_raw = sb("w_raw", [P, 4, KB, D])
        w_hi = sb("w_hi", [P, 4, KB, D], F32R)
        w_lo = sb("w_lo", [P, 4, KB, D], F32R)
        w1 = sb("w1", [P, KB, A])
        b1_col = sb("b1_col", [A, 1])
        v_col = sb("v_col", [A, 1])
        v_wide = sb("v_wide", [A, P])
        bqk_raw = sb("bqk_raw", [P, 2, 2])
        bqk_col = sb("bqk_col", [P, 3, 2])
        bin_col = sb("bin_col", [P, KB, 2])
        bv_wide = sb("bv_wide", [P, D])
        bo_wide = sb("bo_wide", [P, D])
        headsum = sb("headsum", [P, NJ])
        headsum_r = sb("headsum_r", [P, NJ], F32R)
        len_i = sb("len_i", [B, 1], I32)
        len_f = sb("len_f", [B, 1])
        key_pos = sb("key_pos", [B, S])
        mask_row = sb("mask_row", [B, S], F32)
        kind_i = sb("kind_i", [P, B], I32)
        kind_f = sb("kind_f", [P, B])
        is0 = sb("is0", [P, B])
        is1 = sb("is1", [P, B])
        code = sb("code", [P, B])
        rowpos = sb("rowpos", [P, KB])
        side_of = sb("side_of", [P, KB, S])
        cnt = sb("cnt", [P, B, KB])
        cnt_a = sb("cnt_a", [P, KB])
        cnt_b = sb("cnt_b", [P, KB])

        x_sb = sb("x_sb", [P, 2, KB, D])
        s_sb = sb("s_sb", [P, 2, KB, D])
        xt_hi = sb("xt_hi", [P, KB, S], F32R)
        xt_lo = sb("xt_lo", [P, KB, S], F32R)
        st_hi = sb("st_hi", [P, KB, S], F32R)
        st_lo = sb("st_lo", [P, KB, S], F32R)
        q_full = sb("q_full", [P, 2, S])
        k_full = sb("k_full", [P, 2, S])
        q_hi = sb("q_hi", [P, 2, S], F32R)
        q_lo = sb("q_lo", [P, 2, S], F32R)
        k_hi = sb("k_hi", [P, 2, S], F32R)
        k_lo = sb("k_lo", [P, 2, S], F32R)
        prod = sb("prod", [P, 2, S])
        prod_hi = sb("prod_hi", [P, 2, S], F32R)
        prod_lo = sb("prod_lo", [P, 2, S], F32R)
        q_rows = [sb(f"q_rows{i}", [P, NJ, S], F32R) for i in range(2)]
        k_rows = [sb(f"k_rows{i}", [P, NJ, S], F32R) for i in range(2)]
        v_aug = [sb(f"v_aug{i}", [P, KB, H, 32]) for i in range(2)]
        v_self = sb("v_self", [P, 2, KB, D])
        s_self = sb("s_self", [P, 2, KB, H])
        s_max = sb("s_max", [P, 2, KB, H])
        t_max = sb("t_max", [P, 2, KB, H])
        neg_max = sb("neg_max", [P, KB, NG, 2, 2, 2])
        mt_sb = sb("mt_sb", [8, 2, S], F32)
        p_arg = sb("p_arg", [P, KB, H])
        p_self = sb("p_self", [P, KB, H])
        pt = sb("pt", [P, 2 * GRP, KB, S])
        o_sb = sb("o_sb", [P, NG, S])
        vs_p = sb("vs_p", [P, KB, D])
        den = sb("den", [P, KB, H])
        rden = sb("rden", [P, KB, H])
        num = sb("num", [P, KB, D])
        attn = sb("attn", [P, KB, D])
        at_hi = sb("at_hi", [P, KB, S], F32R)
        at_lo = sb("at_lo", [P, KB, S], F32R)
        xr_sb = sb("xr_sb", [P, KB, D])
        x_bo = sb("x_bo", [P, KB, D])
        x1 = sb("x1", [P, KB, D])
        x1t = sb("x1t", [P, KB, S])
        z_sb = sb("z_sb", [A, S])
        hidden = sb("hidden", [P, KB, S])
        masked = sb("masked", [P, KB, S])
        row_max = sb("row_max", [P, KB])
        pool_p = sb("pool_p", [P, KB, S])
        pool_pt = sb("pool_pt", [P, KB, S])
        pool_sum = sb("pool_sum", [P, KB])
        pool_den = sb("pool_den", [P, KB])
        pool_r = sb("pool_r", [P, KB])
        o_out = sb("o_out", [P, KB, D])

        q_spill = nc.dram_tensor("q_spill", [2, 3, P, S], F32).ap()
        k_spill = nc.dram_tensor("k_spill", [2, 3, P, S], F32).ap()
        mask_dram = nc.dram_tensor("mask_dram", [B, S], F32).ap()

        consts_loaded = sem("consts_loaded")
        lens_loaded = sem("lens_loaded")
        weights_loaded = [sem(f"weights_loaded{n}") for n in range(4)]
        pool_zero = sem("pool_zero")
        pool_const = sem("pool_const")
        masks_ready = sem("masks_ready")
        masks_stored = sem("masks_stored")
        dve_const = sem("dve_const")
        w_hi_ready = sem("w_hi_ready")
        w_lo_ready = sem("w_lo_ready")
        bias_ready = sem("bias_ready")
        bias_copied = sem("bias_copied")
        rows_one = sem("rows_one")
        v_zeroed = sem("v_zeroed")
        bias_scaled = sem("bias_scaled")
        x_loaded = [sem(f"x_loaded{i}") for i in range(2)]
        s_loaded = [sem(f"s_loaded{i}") for i in range(2)]
        xr_loaded = sem("xr_loaded")
        xt_ready, xt_hi_done, xt_lo_done = sem("xt_ready"), sem("xt_hi_done"), sem("xt_lo")
        st_ready, st_hi_done, st_lo_done = sem("st_ready"), sem("st_hi_done"), sem("st_lo")
        q_ready, q_full_done, q_copied, q_lo_done = sem("q_ready"), sem("q_full_done"), sem("q_copied"), sem("q_lo_done")
        k_ready, k_full_done, k_copied, k_lo_done = sem("k_ready"), sem("k_full_done"), sem("k_copied"), sem("k_lo_done")
        q_spilled, k_spilled = sem("q_spilled"), sem("k_spilled")
        q_placed, k_placed = sem("q_placed"), sem("k_placed")
        prod_hi_done, prod_lo_done = sem("prod_hi_done"), sem("prod_lo_done")
        ks_ready, prod_done, ss_ready, ss_copied = sem("ks_ready"), sem("prod_done"), sem("ss_ready"), sem("ss_copied")
        v_ready, v_copied, vs_ready, vs_copied = sem("v_ready"), sem("v_copied"), sem("vs_ready"), sem("vs_copied")
        max_scored, max_found = sem("max_scored"), sem("max_found")
        total_max, neg_hi, neg_done = sem("total_max"), sem("neg_hi"), sem("neg_done")
        mt_ready, mt_copied = sem("mt_ready"), sem("mt_copied")
        max_placed = [sem(f"max_placed{g}") for g in range(NG)]
        p_arg_done, p_self_done = sem("p_arg_done"), sem("p_self_done")
        scored, p_ready, pv_ready, pv_copied = sem("scored"), sem("p_ready"), sem("pv_ready"), sem("pv_copied")
        vs_p_done, nat_ready = sem("vs_p_done"), sem("nat_ready")
        den_done, rden_done, num_done, attn_done = sem("den_done"), sem("rden_done"), sem("num_done"), sem("attn_done")
        at_ready, at_hi_done, at_lo_done = sem("at_ready"), sem("at_hi_done"), sem("at_lo")
        wo_ready, x_bo_done, x1_done = sem("wo_ready"), sem("x_bo_done"), sem("x1_done")
        x1t_ready, x1t_copied, z_ready, tanh_done = sem("x1t_ready"), sem("x1t_copied"), sem("z_ready"), sem("tanh_done")
        sb_ready, hidden_done, masked_done, row_max_done = sem("sb_ready"), sem("hidden_done"), sem("masked_done"), sem("row_max_done")
        pool_p_done, pt_ready, pt_copied = sem("pool_p_done"), sem("pt_ready"), sem("pt_copied")
        po_ready, pool_den_done, pool_r_done, out_done, out_stored = (
            sem("po_ready"), sem("pool_den_done"), sem("pool_r_done"), sem("out_done"), sem("out_stored"))

        def live(i, k):
            return not isinstance(i, int) or 0 <= 2 * i + k < B

        def count(i, k, per, done):
            n = i * (2 * per) + (k * per + done)
            return n if not isinstance(i, int) or n > 0 else None

        def row(dram, i, k):
            names = " ".join("abc"[:len(dram.shape) - 1])
            return dram.rearrange(f"(i k) {names} -> i k {names}", k=2)[i + k // 2, k % 2]

        def bank_free(step, i, k):
            at = next(n for n, entry in enumerate(SHARED) if entry[0] == step)
            back = at - BANKS
            while back >= -2 * len(SHARED):
                name, offset, (reader, done) = SHARED[back % len(SHARED)]
                kk = k + back // len(SHARED) + offset
                if live(i, kk):
                    return at % BANKS, sems[reader], count(i, kk, PER_BATCH.get(reader, 1), done)
                back -= BANKS
            return at % BANKS, None, None

        PERIODS = [(n // 2, n % 2) for n in range(-1, B + 2)]
        LOOP_FROM, LOOP_TO = 1, 3
        BEFORE, BODY, AFTER = PERIODS[:4], (1, 2), PERIODS[8:]
        BEFORE_LOADS, BODY_LOADS, AFTER_LOADS = PERIODS[:3], (0, 1), PERIODS[7:]

        x_rows = x.rearrange("b (t p) d -> b p t d", p=P)
        s_rows = side.rearrange("b (t p) d -> b p t d", p=P)
        out_rows = out.rearrange("b (t p) d -> b p t d", p=P)

        block = ctx.enter_context(nc.Block())

        @block.sync
        def _(sp):
            def load(i, k):
                if live(i, k):
                    par = k % 2
                    if (n := count(i, k, 1, -1)) is not None:
                        sp.wait_ge(xt_ready, n)
                    sp.dma_start(x_sb[:, par], row(x_rows, i, k)).then_inc(x_loaded[par], 16)
                    if (n := count(i, k, 1, -1)) is not None:
                        sp.wait_ge(st_ready, n)
                    sp.dma_start(s_sb[:, par], row(s_rows, i, k)).then_inc(s_loaded[par], 16)

            def spill(i, k, hi, lo, lo_done, pattern, dram, placed, placed_per, spilled):
                n_lo = held(count(i, k, 1, 1))
                if (n := held(count(i, k, placed_per, 0))) is not None:
                    sp.wait_ge(placed, n)
                sp.wait_ge(lo_done, n_lo)
                for c, part in enumerate(pattern):
                    src = (hi, lo)[part][:].bitcast(F32)
                    sp.dma_start(dram[:, c].rearrange("e p t -> p e t"), src).then_inc(spilled, 16)

            def held(n):
                return n if n is None or isinstance(n, int) else sp.to_reg(n)

            def place(dram, spilled, n_spilled, rows, placed):
                sp.wait_ge(spilled, n_spilled)
                for e in range(2):
                    sp.dma_start(rows[64 * e:64 * e + ROWS].bitcast(F32),
                                 dram[e].rearrange("c (d j) t -> (c d) j t", d=DH)).then_inc(placed, 16)

            def place_max(i, k, g):
                par = k % 2
                sp.wait_ge(mt_copied, count(i, k, NG, g + 1))
                for e in range(2):
                    sp.dma_start(q_rows[par][64 * e + R_MAX:64 * e + R_MAX + 2, 2 * g:2 * g + 2, :].bitcast(F32),
                                 mt_sb[4 * e:4 * e + 4, g % 2, :]).then_inc(max_placed[g], 16)

            def period(i, k):
                b, nxt, prv = (i, k), (i, k + 1), (i, k - 1)
                if live(*prv):
                    place_max(*prv, 3)
                if live(*nxt):
                    spill(*nxt, q_hi, q_lo, q_lo_done, (0, 0, 1), q_spill, q_placed, 32, q_spilled)
                if live(*b):
                    place_max(*b, 0)
                if live(*nxt):
                    spill(*nxt, k_hi, k_lo, k_lo_done, (0, 1, 0), k_spill, k_placed, 48, k_spilled)
                    par = (k + 1) % 2
                    n_spilled = held(count(*nxt, 48, 48))
                    if (n := held(count(*nxt, H, -H))) is not None:
                        sp.wait_ge(scored, n)
                    else:
                        sp.wait_ge(rows_one, 1)
                    place(q_spill, q_spilled, n_spilled, q_rows[par], q_placed)
                if live(*b):
                    place_max(*b, 1)
                if live(*nxt):
                    place(k_spill, k_spilled, n_spilled, k_rows[par], k_placed)
                    mask = row(mask_dram, *nxt).unsqueeze(0).unsqueeze(0).broadcast_to([2, NJ, S])
                    if isinstance(i, int):
                        sp.wait_ge(masks_stored, 16)
                    sp.dma_start(k_rows[par][R_MASK:R_MASK + 65:64].bitcast(F32), mask).then_inc(k_placed, 16)
                load(i, k + 2)
                if live(*prv):
                    if (n := count(*prv, 1, 0)) is not None:
                        sp.wait_ge(x_bo_done, n)
                    sp.dma_start(xr_sb[:], row(x_rows, *prv)).then_inc(xr_loaded, 16)
                if live(*b):
                    place_max(*b, 2)

            sp.dma_start(s_sb[:, 0], s_rows[0]).then_inc(s_loaded[0], 16)
            sp.dma_start(x_sb[:, 0], x_rows[0]).then_inc(x_loaded[0], 16)
            for n, w in enumerate((Wq, Wk, Wv, Wo)):
                sp.dma_start(w_raw[:, n], w.rearrange("(k p) n -> p k n", p=P)).then_inc(weights_loaded[n], 16)
            sp.dma_start(len_i[:], seq_len.unsqueeze(1)).then_inc(lens_loaded, 16)
            sp.dma_start(kind_i[:], kind.partition_broadcast(P)).then_inc(lens_loaded, 16)
            with nc.allow_non_contiguous_dma("bias vectors, once"):
                for n, vec in enumerate((bq, bk)):
                    sp.dma_start(bqk_raw[:, n, :], vec.rearrange("(j e d) -> d j e", e=2, d=DH)
                                 ).then_inc(consts_loaded, 16)
                for n, vec in enumerate((b_self, b_prev)):
                    sp.dma_start(bin_col[:, :, n], vec.rearrange("a b (k p) -> p (a b k)", p=P)
                                 ).then_inc(consts_loaded, 16)
            sp.dma_start(bv_wide[:], bv.partition_broadcast(P)).then_inc(consts_loaded, 16)
            sp.dma_start(bo_wide[:], bo.partition_broadcast(P)).then_inc(consts_loaded, 16)
            sp.dma_start(w1[:], W1.rearrange("(k p) a -> p k a", p=P)).then_inc(consts_loaded, 16)
            sp.dma_start(b1_col[:], b1.unsqueeze(1)).then_inc(consts_loaded, 16)
            sp.dma_start(v_col[:], v.unsqueeze(1)).then_inc(consts_loaded, 16)
            sp.wait_ge(masks_ready, 1)
            sp.dma_start(mask_dram, mask_row[:]).then_inc(masks_stored, 16)

            for i, k in BEFORE_LOADS:
                period(i, k)
            with sp.Fori(LOOP_FROM, LOOP_TO) as i:
                for k in BODY_LOADS:
                    period(i, k)
            for i, k in AFTER_LOADS:
                period(i, k)
            sp.wait_ge(out_stored, 16 * B)

        @block.gpsimd
        def _(pool):
            nc.gpsimd.memset(ident[:], 0.0).then_inc(pool_zero, 1)
            nc.gpsimd.memset(headsum[:], 0.0).then_inc(pool_zero, 1)
            nc.gpsimd.memset(side_of[:], 0.0).then_inc(pool_zero, 1)
            pool.wait_ge(pool_zero, 3)
            nc.gpsimd.affine_select(out=ident[:], in_=ident[:], compare_op=ALU.not_equal, fill=1.0, base=0,
                                    pattern=[[-1, P]], channel_multiplier=1).then_inc(pool_const, 1)
            nc.gpsimd.iota(key_pos[:], pattern=[[1, S]], base=0, channel_multiplier=0,
                           allow_small_or_imprecise_dtypes=True).then_inc(pool_const, 1)
            for d in range(DH):
                nc.gpsimd.affine_select(out=headsum[:], in_=headsum[:], compare_op=ALU.not_equal, fill=1.0,
                                        base=-NJ * d, pattern=[[-1, NJ]], channel_multiplier=1
                                        ).then_inc(pool_const, 1)
                pool.wait_ge(pool_const, 3 + d)
            nc.gpsimd.iota(rowpos[:], pattern=[[P, KB]], base=0, channel_multiplier=1,
                           allow_small_or_imprecise_dtypes=True).then_inc(pool_const, 1)
            nc.gpsimd.affine_select(out=side_of[:], in_=side_of[:], compare_op=ALU.is_ge, fill=1.0, base=0,
                                    pattern=[[P, KB], [-1, S]], channel_multiplier=1).then_inc(pool_const, 1)
            pool.wait_ge(pool_const, 4 + DH)
            nc.gpsimd.affine_select(out=side_of[:], in_=side_of[:], compare_op=ALU.is_ge, fill=-1.0, base=0,
                                    pattern=[[-P, KB], [1, S]], channel_multiplier=-1).then_inc(pool_const, 1)


            for par in range(2):
                nc.gpsimd.memset(q_rows[par][:].bitcast(F32), 1.0)
                last = nc.gpsimd.memset(k_rows[par][:].bitcast(F32), 1.0)
            last.then_inc(rows_one, 1)

            def split_lo(i, k, full_done, hi_done, full, hi, lo, lo_done, spilled):
                pool.wait_ge(full_done, count(i, k, 1, 1))
                pool.wait_ge(hi_done, count(i, k, 1, 1))
                if (n := count(i, k, 48, 0)) is not None:
                    pool.wait_ge(spilled, n)
                nc.gpsimd.tensor_tensor(lo[:], full[:], hi[:].bitcast(F32), ALU.subtract).then_inc(lo_done, 1)

            def period(i, k):
                b, nxt, prv = (i, k), (i, k + 1), (i, k - 1)
                if live(*prv):
                    par = (k - 1) % 2
                    pool.wait_ge(p_self_done, count(*prv, 1, 1))
                    pool.wait_ge(vs_copied, count(*prv, 1, 1))
                    if (n := count(*prv, 2, 0)) is not None:
                        pool.wait_ge(num_done, n)
                    for t in range(KB):
                        last = nc.gpsimd.tensor_tensor(
                            vs_p[:, t].rearrange("p (h d) -> p h d", d=DH),
                            v_self[:, par, t].rearrange("p (h d) -> p h d", d=DH),
                            p_self[:, t].unsqueeze(2).broadcast_to([P, H, DH]), ALU.mult)
                    last.then_inc(vs_p_done, 1)
                if live(*nxt):
                    split_lo(*nxt, q_full_done, q_copied, q_full, q_hi, q_lo, q_lo_done, q_spilled)
                    split_lo(*nxt, k_full_done, k_copied, k_full, k_hi, k_lo, k_lo_done, k_spilled)
                    pool.wait_ge(prod_hi_done, count(*nxt, 1, 1))
                    if (n := count(*nxt, 1, 0)) is not None:
                        pool.wait_ge(ss_ready, n)
                    nc.gpsimd.tensor_tensor(prod_lo[:], prod[:], prod_hi[:].bitcast(F32), ALU.subtract
                                            ).then_inc(prod_lo_done, 1)
                if live(*prv):
                    if (n := count(*prv, 1, 0)) is not None:
                        pool.wait_ge(at_ready, n)
                    for t in range(KB):
                        pool.wait_ge(num_done, count(*prv, 2, t + 1))
                        nc.gpsimd.tensor_tensor(
                            attn[:, t].rearrange("p (h d) -> p h d", d=DH),
                            num[:, t].rearrange("p (h d) -> p h d", d=DH),
                            rden[:, t].unsqueeze(2).broadcast_to([P, H, DH]), ALU.mult).then_inc(attn_done, 1)
                    pool.wait_ge(xr_loaded, count(*prv, 16, 16))
                    if (n := count(*prv, 1, 0)) is not None:
                        pool.wait_ge(x1_done, n)
                    nc.gpsimd.tensor_tensor(x_bo[:], xr_sb[:], bo_wide[:].unsqueeze(1).broadcast_to([P, KB, D]),
                                            ALU.add).then_inc(x_bo_done, 1)

            for i, k in BEFORE:
                period(i, k)
            with pool.Fori(LOOP_FROM, LOOP_TO) as i:
                for k in BODY:
                    period(i, k)
            for i, k in AFTER:
                period(i, k)

        @block.scalar
        def _(act):
            def scalar_max_t(i, k, g):
                act.wait_ge(mt_ready, count(i, k, NG, g + 1))
                if g >= 2:
                    act.wait_ge(max_placed[g - 2], count(i, k, 32, 32))
                elif (n := count(i, k, 32, 0)) is not None:
                    act.wait_ge(max_placed[g + 2], n)
                bank = bank_free(f"MT{g}", i, k)[0]
                nc.scalar.activation(mt_sb[:, g % 2, :], ps_any[0:8, bank, 0, :], ACT.Copy).then_inc(mt_copied, 1)

            def exps(i, k, h):
                act.wait_ge(scored, count(i, k, H, h + 1))
                if (n := count(i, k, NG, h // GRP - 1)) is not None:
                    act.wait_ge(pv_ready, n)
                nc.scalar.activation(pt[:, h % 8], ps_exp[:, h % 2], ACT.Exp).then_inc(p_ready, 1)

            def pv_copy(i, k, g):
                act.wait_ge(pv_ready, count(i, k, NG, g + 1))
                if (n := count(i, k, 2, 0)) is not None:
                    act.wait_ge(nat_ready, n)
                nc.scalar.activation(o_sb[:, g], ps_pv[:, 0, :], ACT.Copy).then_inc(pv_copied, 1)

            for n in range(4):
                act.wait_ge(weights_loaded[n], 16)
                for kb in range(KB):
                    dst, src = w_hi[:, n, kb], w_raw[:, n, kb]
                    if n < 2:
                        dst = dst.rearrange("p (e d j) -> p e d j", e=2, d=DH)
                        src = src.rearrange("p (j e d) -> p e d j", e=2, d=DH)
                    nc.scalar.activation(dst, src, ACT.Copy, scale=QSCALE if n == 0 else 1.0
                                         ).then_inc(w_hi_ready, 1)

            def period(i, k):
                b, nxt, prv, old = (i, k), (i, k + 1), (i, k - 1), (i, k - 2)
                for s in range(SLOTS):
                    g = {1: 1, 5: 2, 9: 3, 13: 0}.get(s)
                    who = b if g == 0 else prv
                    if g is not None and live(*who):
                        pv_copy(*who, g)
                    if s == 1 and live(*nxt):
                        act.wait_ge(st_ready, count(*nxt, 1, 1))
                        if (n := count(*nxt, 1, 0)) is not None:
                            act.wait_ge(vs_ready, n)
                        nc.scalar.activation(st_hi[:], ps_any[:, bank_free("TS", i, k)[0]], ACT.Copy
                                             ).then_inc(st_hi_done, 1)
                    if s == 1 and live(*prv):
                        scalar_max_t(*prv, 3)
                        act.wait_ge(p_arg_done, count(*prv, 1, 1))
                        if (n := count(*prv, 1, 0)) is not None:
                            act.wait_ge(vs_p_done, n)
                            act.wait_ge(den_done, count(*prv, 2, 0))
                        nc.scalar.activation(p_self[:], p_arg[:], ACT.Exp).then_inc(p_self_done, 1)
                    if s == 3 and live(*nxt):
                        act.wait_ge(xt_ready, count(*nxt, 1, 1))
                        if (n := count(*nxt, 1, 0)) is not None:
                            act.wait_ge(v_ready, n)
                        nc.scalar.activation(xt_hi[:], ps_any[:, bank_free("TX", i, k)[0]], ACT.Copy
                                             ).then_inc(xt_hi_done, 1)
                    if s == 4 and live(*nxt):
                        qk_copy(*nxt, "Q", i, k)
                    if s == 5 and live(*old):
                        act.wait_ge(x1t_ready, count(*old, 1, 1))
                        if (n := count(*old, 1, 0)) is not None:
                            act.wait_ge(z_ready, n)
                        nc.scalar.activation(x1t[:], ps_any[:, bank_free("X1T", i, k)[0]], ACT.Copy
                                             ).then_inc(x1t_copied, 1)
                    if s == 6:
                        if live(*b):
                            scalar_max_t(*b, 0)
                        if live(*nxt):
                            qk_copy(*nxt, "K", i, k)
                    if s == 7 and live(*old):
                        act.wait_ge(z_ready, count(*old, 1, 1))
                        if (n := count(*old, 1, 0)) is not None:
                            act.wait_ge(sb_ready, n)
                        nc.scalar.activation(z_sb[:], ps_any[0:A, bank_free("Z", i, k)[0], 0, :], ACT.Tanh,
                                             bias=b1_col[:, 0:1]).then_inc(tanh_done, 1)
                    if s == 10:
                        if live(*b):
                            scalar_max_t(*b, 1)
                        if live(*old):
                            act.wait_ge(row_max_done, count(*old, 1, 1))
                            if (n := count(*old, 1, 0)) is not None:
                                act.wait_ge(pt_ready, n)
                                act.wait_ge(pool_den_done, n)
                            for t in range(KB):
                                nc.scalar.activation(pool_p[:, t], masked[:, t], ACT.Exp,
                                                     bias=row_max[:, t:t + 1], accum_out=pool_sum[:, t:t + 1]
                                                     ).then_inc(pool_p_done, 1)
                    if s == 13:
                        if live(*old):
                            act.wait_ge(pt_ready, count(*old, 1, 1))
                            if (n := count(*old, 1, 0)) is not None:
                                act.wait_ge(po_ready, n)
                            nc.scalar.activation(pool_pt[:], ps_any[:, bank_free("PT", i, k)[0]], ACT.Copy
                                                 ).then_inc(pt_copied, 1)
                        if live(*nxt):
                            par = (k + 1) % 2
                            act.wait_ge(ss_ready, count(*nxt, 1, 1))
                            if (n := count(*nxt, 1, -1)) is not None:
                                act.wait_ge(p_arg_done, n)
                            nc.scalar.activation(
                                s_self[:, par].rearrange("p t (j e) -> p t j e", e=2),
                                ps_any[:, bank_free("SS", i, k)[0], 0, 0:2 * H].rearrange(
                                    "p (t e j) -> p t j e", t=KB, e=2), ACT.Copy).then_inc(ss_copied, 1)
                    if s == 14 and live(*b):
                        scalar_max_t(*b, 2)
                    if s == 15:
                        if live(*prv):
                            act.wait_ge(at_ready, count(*prv, 1, 1))
                            if (n := count(*prv, 1, 0)) is not None:
                                act.wait_ge(wo_ready, n)
                            nc.scalar.activation(at_hi[:], ps_any[:, bank_free("AT", i, k)[0]], ACT.Copy
                                                 ).then_inc(at_hi_done, 1)
                        if live(*old):
                            act.wait_ge(out_done, count(*old, 1, 1))
                            act.dma_start(row(out_rows, *old), o_out[:]).then_inc(out_stored, 16)
                    who = b if s >= LAG else prv
                    if live(*who):
                        exps(*who, (s - LAG) % SLOTS)

            def qk_copy(i, k, step, pi, pk):
                ready, full, hi, full_done, hi_done, lo_done, spilled, n_bias = {
                    "Q": (q_ready, q_full, q_hi, q_full_done, q_copied, q_lo_done, q_spilled, 0),
                    "K": (k_ready, k_full, k_hi, k_full_done, k_copied, k_lo_done, k_spilled, 1)}[step]
                bank = bank_free(step, pi, pk)[0]
                act.wait_ge(ready, count(i, k, 1, 1))
                if (n := count(i, k, 1, 0)) is not None:
                    act.wait_ge(lo_done, n)
                    if step == "Q":
                        act.wait_ge(prod_done, n)
                else:
                    act.wait_ge(bias_copied, 1)
                for m in range(2):
                    last = nc.scalar.activation(full[:, m], ps_any[:, bank, m], ACT.Identity,
                                                bias=bqk_col[:, n_bias, m:m + 1])
                last.then_inc(full_done, 1)
                if (n := count(i, k, 48, 0)) is not None:
                    act.wait_ge(spilled, n)
                for m in range(2):
                    last = nc.scalar.activation(hi[:, m], ps_any[:, bank, m], ACT.Identity,
                                                bias=bqk_col[:, n_bias, m:m + 1])
                last.then_inc(hi_done, 1)

            for i, k in BEFORE:
                period(i, k)
            with act.Fori(LOOP_FROM, LOOP_TO) as i:
                for k in BODY:
                    period(i, k)
            for i, k in AFTER:
                period(i, k)

        @block.vector
        def _(dve):
            def setup_biases():
                dve.wait_ge(consts_loaded, 9 * 16)
                nc.vector.tensor_scalar(bqk_raw[:, 0], bqk_raw[:, 0], QSCALE, None, ALU.mult
                                        ).then_inc(bias_scaled, 1)
                dve.wait_ge(bias_scaled, 1)
                dve.wait_ge(bias_ready, 1)
                for n, b_of in enumerate((0, 1, 1)):
                    last = nc.vector.tensor_tensor(bqk_col[:, n], ps_max[:, 0, 0, 2 * n:2 * n + 2],
                                                   bqk_raw[:, b_of], ALU.add)
                last.then_inc(bias_copied, 1)

            for n in range(4):
                for kb in range(KB):
                    dve.wait_ge(w_hi_ready, KB * n + kb + 1)
                    if n < 2:
                        for e in range(2):
                            hi, lo = (w[:, n, kb].rearrange("p (e d j) -> p e d j", e=2, d=DH)[:, e]
                                      for w in (w_hi, w_lo))
                            src = w_raw[:, n, kb].rearrange("p (j e d) -> p e d j", e=2, d=DH)[:, e]
                            nc.vector.scalar_tensor_tensor(out=lo, in0=src, scalar=QSCALE if n == 0 else 1.0,
                                                           in1=hi.bitcast(F32), op0=ALU.mult, op1=ALU.subtract
                                                           ).then_inc(w_lo_ready, 1)
                    else:
                        nc.vector.tensor_tensor(w_lo[:, n, kb], w_raw[:, n, kb], w_hi[:, n, kb].bitcast(F32),
                                                ALU.subtract).then_inc(w_lo_ready, 1)
                if n == 1:
                    setup_biases()
            for par in range(2):
                last = nc.vector.memset(v_aug[par][:], 0.0)
            last.then_inc(v_zeroed, 1)
            nc.vector.memset(zeros[:], 0.0).then_inc(v_zeroed, 1)
            dve.wait_ge(lens_loaded, 32)
            dve.wait_ge(v_zeroed, 2)
            dve.wait_ge(consts_loaded, 9 * 16)
            for par in range(2):
                nc.vector.memset(v_aug[par][:, :, :, DH:DH + 1], 1.0)
            nc.vector.tensor_copy(len_f[:], len_i[:]).then_inc(dve_const, 1)
            nc.vector.tensor_copy(kind_f[:], kind_i[:]).then_inc(dve_const, 1)
            nc.vector.tensor_scalar(v_wide[:], zeros[0:A, :], v_col[:, 0:1], None, ALU.add).then_inc(dve_const, 1)
            dve.wait_ge(dve_const, 3)
            dve.wait_ge(pool_const, 5 + DH)
            nc.vector.tensor_scalar(mask_row[:], key_pos[:], len_f[:, 0:1], MASKED, ALU.is_ge, ALU.mult
                                    ).then_inc(masks_ready, 1)
            nc.vector.tensor_scalar(is0[:], kind_f[:], 0.0, None, ALU.is_equal).then_inc(dve_const, 1)
            nc.vector.tensor_scalar(is1[:], kind_f[:], 1.0, None, ALU.is_equal).then_inc(dve_const, 1)
            dve.wait_ge(dve_const, 5)
            nc.vector.tensor_tensor(code[:], is0[:], is1[:], ALU.subtract).then_inc(dve_const, 1)
            nc.vector.tensor_scalar(cnt_a[:], rowpos[:], float(2 - S), None, ALU.add).then_inc(dve_const, 1)
            nc.vector.tensor_scalar(cnt_b[:], rowpos[:], -1.0, 1.0, ALU.mult, ALU.add).then_inc(dve_const, 1)
            nc.vector.memset(cnt[:], float(S - 1)).then_inc(dve_const, 1)
            n_const = 9
            dve.wait_ge(dve_const, n_const)
            for sel, diff in ((is0, cnt_a), (is1, cnt_b)):
                for t in range(KB):
                    nc.vector.scalar_tensor_tensor(out=cnt[:, :, t], in0=sel[:], scalar=diff[:, t:t + 1],
                                                   in1=cnt[:, :, t], op0=ALU.mult, op1=ALU.add
                                                   ).then_inc(dve_const, 1)
                n_const += KB
                dve.wait_ge(dve_const, n_const)
            nc.vector.tensor_copy(headsum_r[:], headsum[:]).then_inc(dve_const, 1)

            def max_of(i, k, h):
                dve.wait_ge(max_scored, count(i, k, H, h + 1))
                nc.vector.tensor_reduce(s_max[:, k % 2, :, h], ps_max[:, h % 2], AX.X, ALU.max
                                        ).then_inc(max_found, 1)

            def group_max(i, k, g):
                par = k % 2
                heads = slice(GRP * g, GRP * g + GRP)
                dve.wait_ge(max_found, count(i, k, H, GRP * (g + 1)))
                dve.wait_ge(ss_copied, count(i, k, 1, 1))
                nc.vector.tensor_tensor(t_max[:, par, :, heads], s_max[:, par, :, heads],
                                        s_self[:, par, :, heads], ALU.max).then_inc(total_max, 1)
                dve.wait_ge(total_max, count(i, k, NG, g + 1))
                if (n := count(i, k, NG, g + 1 - NG)) is not None:
                    dve.wait_ge(mt_ready, n)
                for t in range(KB):
                    top = t_max[:, par, t, heads].rearrange("p (j e) -> p e j", e=2)
                    last = nc.vector.tensor_scalar(neg_max[:, t, g, :, 0].bitcast(F32R), top, -1.0, None, ALU.mult)
                last.then_inc(neg_hi, 1)
                dve.wait_ge(neg_hi, count(i, k, NG, g + 1))
                for t in range(KB):
                    top = t_max[:, par, t, heads].rearrange("p (j e) -> p e j", e=2)
                    last = nc.vector.scalar_tensor_tensor(out=neg_max[:, t, g, :, 1].bitcast(F32R), in0=top,
                                                          scalar=-1.0, in1=neg_max[:, t, g, :, 0],
                                                          op0=ALU.mult, op1=ALU.subtract)
                last.then_inc(neg_done, 1)

            def period(i, k):
                b, nxt, prv, old = (i, k), (i, k + 1), (i, k - 1), (i, k - 2)
                for s in range(SLOTS):
                    if s == 0:
                        if live(*prv):
                            group_max(*prv, 3)
                            if (n := count(*prv, 1, 0)) is not None:
                                dve.wait_ge(p_self_done, n)
                            nc.vector.tensor_tensor(p_arg[:], s_self[:, (k - 1) % 2], t_max[:, (k - 1) % 2],
                                                    ALU.subtract).then_inc(p_arg_done, 1)
                        if live(*b):
                            dve.wait_ge(vs_ready, count(*b, 1, 1))
                            if (n := count(*b, 1, -1)) is not None:
                                dve.wait_ge(vs_p_done, n)
                            nc.vector.tensor_tensor(v_self[:, k % 2], ps_any[:, bank_free("VS", i, k)[0]],
                                                    bv_wide[:].unsqueeze(1).broadcast_to([P, KB, D]), ALU.add
                                                    ).then_inc(vs_copied, 1)
                    if s == 1 and live(*nxt):
                        dve.wait_ge(st_hi_done, count(*nxt, 1, 1))
                        nc.vector.tensor_tensor(st_lo[:], ps_any[:, bank_free("TS", i, k)[0]],
                                                st_hi[:].bitcast(F32), ALU.subtract).then_inc(st_lo_done, 1)
                    if s == 2 and live(*old):
                        dve.wait_ge(wo_ready, count(*old, 1, 1))
                        dve.wait_ge(x_bo_done, count(*old, 1, 1))
                        if (n := count(*old, 1, 0)) is not None:
                            dve.wait_ge(out_done, n)
                        nc.vector.tensor_tensor(x1[:], ps_any[:, bank_free("WO", i, k)[0]], x_bo[:], ALU.add
                                                ).then_inc(x1_done, 1)
                    if s == 3 and live(*nxt):
                        dve.wait_ge(xt_hi_done, count(*nxt, 1, 1))
                        nc.vector.tensor_tensor(xt_lo[:], ps_any[:, bank_free("TX", i, k)[0]],
                                                xt_hi[:].bitcast(F32), ALU.subtract).then_inc(xt_lo_done, 1)
                    if s in (4, 8, 12) and live(*b):
                        group_max(*b, s // 4 - 1)
                    if s == 7 and live(*old):
                        kk = k - 2
                        codes = code[:].rearrange("p (i k) -> p i k", k=2)
                        if (n := count(*old, 1, 0)) is not None:
                            dve.wait_ge(masked_done, n)
                        nc.vector.tensor_scalar(hidden[:], side_of[:], codes[:, i + kk // 2, kk % 2:kk % 2 + 1],
                                                MASKED, ALU.is_equal, ALU.mult).then_inc(hidden_done, 1)
                    if s == 8 and live(*nxt):
                        dve.wait_ge(ks_ready, count(*nxt, 1, 1))
                        dve.wait_ge(q_full_done, count(*nxt, 1, 1))
                        if (n := count(*nxt, 1, 0)) is not None:
                            dve.wait_ge(prod_lo_done, n)
                        for m in range(2):
                            last = nc.vector.scalar_tensor_tensor(
                                out=prod[:, m], in0=ps_any[:, bank_free("KS", i, k)[0], m],
                                scalar=bqk_col[:, 2, m:m + 1], in1=q_full[:, m], op0=ALU.add, op1=ALU.mult)
                        last.then_inc(prod_done, 1)
                        dve.wait_ge(prod_done, count(*nxt, 1, 1))
                        if (n := count(*nxt, 1, 0)) is not None:
                            dve.wait_ge(ss_ready, n)
                        nc.vector.tensor_copy(prod_hi[:], prod[:]).then_inc(prod_hi_done, 1)
                    if s == 9 and live(*old):
                        dve.wait_ge(sb_ready, count(*old, 1, 1))
                        dve.wait_ge(hidden_done, count(*old, 1, 1))
                        if (n := count(*old, 2, 0)) is not None:
                            dve.wait_ge(pool_p_done, n)
                        nc.vector.tensor_tensor(
                            masked[:], hidden[:],
                            ps_any[:, bank_free("SB", i, k)[0], 0].unsqueeze(1).broadcast_to([P, KB, S]),
                            ALU.add).then_inc(masked_done, 1)
                        dve.wait_ge(masked_done, count(*old, 1, 1))
                        nc.vector.tensor_reduce(row_max[:], masked[:], AX.X, ALU.max, negate=True
                                                ).then_inc(row_max_done, 1)
                    if s == 10 and live(*nxt):
                        dve.wait_ge(v_ready, count(*nxt, 1, 1))
                        if (n := count(*nxt, NG, -NG)) is not None:
                            dve.wait_ge(pv_ready, n)
                        for t in range(KB):
                            last = nc.vector.tensor_tensor(
                                v_aug[(k + 1) % 2][:, t, :, 0:DH],
                                ps_any[:, bank_free("V", i, k)[0], t].rearrange("p (h d) -> p h d", d=DH),
                                bv_wide[:].rearrange("p (h d) -> p h d", d=DH), ALU.add)
                        last.then_inc(v_copied, 1)
                    if s == 12 and live(*prv):
                        for t in range(KB):
                            bank = ps_any[:, bank_free(f"NAT{t}", i, k)[0]].rearrange(
                                "p t (h c) -> p (t h) c", c=32)
                            dve.wait_ge(nat_ready, count(*prv, 2, t + 1))
                            dve.wait_ge(p_self_done, count(*prv, 1, 1))
                            if (n := count(*prv, 2, t - 1)) is not None:
                                dve.wait_ge(attn_done, n)
                            nc.vector.tensor_tensor(den[:, t], bank[:, :, DH], p_self[:, t], ALU.add
                                                    ).then_inc(den_done, 1)
                            dve.wait_ge(den_done, count(*prv, 2, t + 1))
                            nc.vector.reciprocal(rden[:, t], den[:, t]).then_inc(rden_done, 1)
                            dve.wait_ge(vs_p_done, count(*prv, 1, 1))
                            dve.wait_ge(rden_done, count(*prv, 2, t + 1))
                            nc.vector.tensor_tensor(
                                num[:, t].rearrange("p (h d) -> p h d", d=DH), bank[:, :, 0:DH],
                                vs_p[:, t].rearrange("p (h d) -> p h d", d=DH), ALU.add).then_inc(num_done, 1)
                    if s == 14 and live(*old):
                        dve.wait_ge(pool_p_done, count(*old, 2, 2))
                        kk = k - 2
                        rows_cnt = cnt[:].rearrange("p (i k) t -> p i k t", k=2)[:, i + kk // 2, kk % 2]
                        nc.vector.tensor_tensor(pool_den[:], pool_sum[:], rows_cnt, ALU.mult
                                                ).then_inc(pool_den_done, 1)
                        dve.wait_ge(pool_den_done, count(*old, 1, 1))
                        nc.vector.reciprocal(pool_r[:], pool_den[:]).then_inc(pool_r_done, 1)
                        dve.wait_ge(pool_r_done, count(*old, 1, 1))
                        dve.wait_ge(po_ready, count(*old, 1, 1))
                        if (n := count(*old, 16, 0)) is not None:
                            dve.wait_ge(out_stored, n)
                        for t in range(KB):
                            last = nc.vector.scalar_tensor_tensor(
                                out=o_out[:, t], in0=ps_any[:, bank_free("PO", i, k)[0], t],
                                scalar=pool_r[:, t:t + 1], in1=x1[:, t], op0=ALU.mult, op1=ALU.add)
                        last.then_inc(out_done, 1)
                    if s == 15 and live(*prv):
                        dve.wait_ge(at_hi_done, count(*prv, 1, 1))
                        nc.vector.tensor_tensor(at_lo[:], ps_any[:, bank_free("AT", i, k)[0]],
                                                at_hi[:].bitcast(F32), ALU.subtract).then_inc(at_lo_done, 1)
                    if live(*b):
                        max_of(*b, s)

            for i, k in BEFORE:
                period(i, k)
            with dve.Fori(LOOP_FROM, LOOP_TO) as i:
                for k in BODY:
                    period(i, k)
            for i, k in AFTER:
                period(i, k)

        @block.tensor
        def _(pe):
            def products(out_of, hi, lo, n, stationary_w):
                for m in range(2):
                    terms = [(kb, a, c) for kb in range(KB) for a, c in ((0, 0), (0, 1), (1, 0))]
                    for j, (kb, a, c) in enumerate(terms):
                        act_part, w_part = (hi, lo)[a], (w_hi, w_lo)[c]
                        if stationary_w:
                            lhs, rhs = w_part[:, n, kb, P * m:P * m + P], act_part[:, kb, :]
                        else:
                            lhs, rhs = act_part[:, kb, P * m:P * m + P], w_part[:, n, kb, :]
                        last = pe.matmul(out_of[:, m], lhs, rhs, start=(j == 0), stop=(j == len(terms) - 1))
                return last

            def transposed(out_of, src):
                for kb in range(KB):
                    for t in range(KB):
                        last = pe.transpose(out_of[:, kb, P * t:P * t + P], src[:, t, P * kb:P * kb + P], ident[:])
                return last

            def take_bank(step, i, k):
                bank, reader, n = bank_free(step, i, k)
                if n is not None:
                    pe.wait_ge(reader, n)
                return ps_any[:, bank]

            def score_for_max(i, k, h):
                par, e, j = k % 2, h % 2, h // 2
                if h == 0:
                    pe.wait_ge(q_placed, count(i, k, 32, 32))
                    pe.wait_ge(k_placed, count(i, k, 48, 48))
                if (n := count(i, k, H, h - 1)) is not None:
                    pe.wait_ge(max_found, n)
                rows = slice(64 * e, 64 * e + KM)
                for t in range(KB):
                    last = pe.matmul(ps_max[:, e, t], q_rows[par][rows, j, P * t:P * t + P],
                                     k_rows[par][rows, j, :], start=True, stop=True)
                last.then_inc(max_scored, 1)

            def score_for_exp(i, k, h):
                par, e, j = k % 2, h % 2, h // 2
                if h % GRP == 0:
                    pe.wait_ge(max_placed[h // GRP], count(i, k, 32, 32))
                if (n := count(i, k, H, h - 1)) is not None:
                    pe.wait_ge(p_ready, n)
                rows = slice(64 * e, 64 * e + KF)
                for t in range(KB):
                    last = pe.matmul(ps_exp[:, e, t], k_rows[par][rows, j, P * t:P * t + P],
                                     q_rows[par][rows, j, :], start=True, stop=True)
                last.then_inc(scored, 1)

            def pv(i, k, g):
                par = k % 2
                pe.wait_ge(p_ready, count(i, k, H, GRP * (g + 1)))
                if g == 0:
                    pe.wait_ge(v_copied, count(i, k, 1, 1))
                if (n := count(i, k, NG, g)) is not None:
                    pe.wait_ge(pv_copied, n)
                for t in range(KB):
                    for c in range(GRP):
                        h = GRP * g + c
                        last = pe.matmul(ps_pv[32 * c:32 * c + 32, 0, :], v_aug[par][:, t, h, :],
                                         pt[:, h % 8, t, :], start=(t == 0), stop=(t == KB - 1),
                                         skip_group_check=True)
                last.then_inc(pv_ready, 1)

            def max_to_rows(i, k, g, pi, pk):
                bank = take_bank(f"MT{g}", pi, pk)
                pe.wait_ge(neg_done, count(i, k, NG, g + 1))
                for t in range(KB):
                    last = pe.transpose(bank[0:8, 0, P * t:P * t + P],
                                        neg_max[:, t, g].rearrange("p e c j -> p (e c j)"), ident[:])
                last.then_inc(mt_ready, 1)

            def biases():
                pe.wait_ge(w_lo_ready, 8)
                pe.wait_ge(consts_loaded, 9 * 16)
                for n, (w_of, b_of) in enumerate(((0, 0), (1, 1), (1, 0))):
                    for m in range(2):
                        terms = [(part, kb) for part in (w_hi, w_lo) for kb in range(KB)]
                        for j, (part, kb) in enumerate(terms):
                            last = pe.matmul(ps_max[:, 0, 0, 2 * n + m:2 * n + m + 1],
                                             part[:, w_of, kb, P * m:P * m + P].bitcast(F32),
                                             bin_col[:, kb, b_of:b_of + 1], start=(j == 0), stop=(j == 3))
                last.then_inc(bias_ready, 1)

            def period(i, k):
                b, nxt, prv, old = (i, k), (i, k + 1), (i, k - 1), (i, k - 2)
                for s in range(SLOTS):
                    if live(*b):
                        score_for_max(*b, s)
                    who = b if s >= LAG else prv
                    if live(*who):
                        score_for_exp(*who, (s - LAG) % SLOTS)
                    g = {12: 0, 0: 1, 4: 2, 8: 3}.get(s)
                    who = b if g == 0 else prv
                    if g is not None and live(*who):
                        pv(*who, g)
                    if s == 0:
                        if live(*nxt):
                            bank = take_bank("TS", i, k)
                            pe.wait_ge(s_loaded[(k + 1) % 2], count(i + (k + 1) // 2, 0, 8, 16))
                            transposed(bank, s_sb[:, (k + 1) % 2]).then_inc(st_ready, 1)
                        if live(*prv):
                            max_to_rows(*prv, 3, i, k)
                    if s == 1 and live(*old):
                        bank = take_bank("WO", i, k)
                        pe.wait_ge(at_hi_done, count(*old, 1, 1))
                        pe.wait_ge(at_lo_done, count(*old, 1, 1))
                        products(bank, at_hi, at_lo, 3, False).then_inc(wo_ready, 1)
                    if s == 2 and live(*nxt):
                        if not live(*b):
                            biases()
                        bank = take_bank("TX", i, k)
                        pe.wait_ge(x_loaded[(k + 1) % 2], count(i + (k + 1) // 2, 0, 8, 16))
                        transposed(bank, x_sb[:, (k + 1) % 2]).then_inc(xt_ready, 1)
                    if s == 3 and live(*nxt):
                        bank = take_bank("Q", i, k)
                        pe.wait_ge(st_hi_done, count(*nxt, 1, 1))
                        pe.wait_ge(st_lo_done, count(*nxt, 1, 1))
                        products(bank, st_hi, st_lo, 0, True).then_inc(q_ready, 1)
                    if s == 4 and live(*old):
                        bank = take_bank("X1T", i, k)
                        pe.wait_ge(x1_done, count(*old, 1, 1))
                        transposed(bank, x1).then_inc(x1t_ready, 1)
                    if s == 5:
                        if live(*b):
                            max_to_rows(*b, 0, i, k)
                        if live(*nxt):
                            bank = take_bank("K", i, k)
                            pe.wait_ge(xt_hi_done, count(*nxt, 1, 1))
                            pe.wait_ge(xt_lo_done, count(*nxt, 1, 1))
                            products(bank, xt_hi, xt_lo, 1, True).then_inc(k_ready, 1)
                    if s == 6 and live(*old):
                        bank = take_bank("Z", i, k)
                        pe.wait_ge(x1t_copied, count(*old, 1, 1))
                        for kb in range(KB):
                            last = pe.matmul(bank[0:A, 0], w1[:, kb, :], x1t[:, kb, :],
                                             start=(kb == 0), stop=(kb == KB - 1))
                        last.then_inc(z_ready, 1)
                    if s == 7 and live(*nxt):
                        bank = take_bank("KS", i, k)
                        products(bank, st_hi, st_lo, 1, True).then_inc(ks_ready, 1)
                    if s == 8 and live(*old):
                        bank = take_bank("SB", i, k)
                        pe.wait_ge(tanh_done, count(*old, 1, 1))
                        pe.matmul(bank[:, 0], v_wide[:], z_sb[:], start=True, stop=True).then_inc(sb_ready, 1)
                    if s == 9:
                        if live(*b):
                            max_to_rows(*b, 1, i, k)
                        if live(*nxt):
                            bank = take_bank("V", i, k)
                            if not live(*b):
                                pe.wait_ge(w_lo_ready, 12)
                            products(bank, xt_hi, xt_lo, 2, False).then_inc(v_ready, 1)
                    if s == 11 and live(*prv):
                        for t in range(KB):
                            bank = take_bank(f"NAT{t}", i, k)
                            pe.wait_ge(pv_copied, count(*prv, NG, NG))
                            for gg in range(NG):
                                last = pe.transpose(bank[:, gg // 2, P * (gg % 2):P * (gg % 2) + P],
                                                    o_sb[:, gg, P * t:P * t + P], ident[:])
                            last.then_inc(nat_ready, 1)
                    if s == 12:
                        if live(*old):
                            bank = take_bank("PT", i, k)
                            pe.wait_ge(pool_p_done, count(*old, 2, 2))
                            transposed(bank, pool_p).then_inc(pt_ready, 1)
                        if live(*nxt):
                            bank = take_bank("SS", i, k)
                            pe.wait_ge(prod_lo_done, count(*nxt, 1, 1))
                            if not live(*b):
                                pe.wait_ge(dve_const, 14)
                            for t in range(KB):
                                for e in range(2):
                                    at = NJ * (2 * t + e)
                                    for part in (prod_hi, prod_lo):
                                        last = pe.matmul(bank[:, 0, at:at + NJ], part[:, e, P * t:P * t + P],
                                                         headsum_r[:], start=(part is prod_hi),
                                                         stop=(part is prod_lo))
                            last.then_inc(ss_ready, 1)
                    if s == 13:
                        if live(*b):
                            max_to_rows(*b, 2, i, k)
                        if live(*old):
                            bank = take_bank("PO", i, k)
                            pe.wait_ge(pt_copied, count(*old, 1, 1))
                            for t in range(KB):
                                for kb in range(KB):
                                    last = pe.matmul(bank[:, t], pool_pt[:, kb, P * t:P * t + P], x1[:, kb, :],
                                                     start=(kb == 0), stop=(kb == KB - 1))
                            last.then_inc(po_ready, 1)
                    if s == 14 and live(*prv):
                        bank = take_bank("AT", i, k)
                        pe.wait_ge(attn_done, count(*prv, 2, 2))
                        transposed(bank, attn).then_inc(at_ready, 1)
                    if s == 15 and live(*nxt):
                        bank = take_bank("VS", i, k)
                        products(bank, st_hi, st_lo, 2, False).then_inc(vs_ready, 1)

            pe.wait_ge(pool_const, 1)

            for i, k in BEFORE:
                period(i, k)
            with pe.Fori(LOOP_FROM, LOOP_TO) as i:
                for k in BODY:
                    period(i, k)
            for i, k in AFTER:
                period(i, k)


_INS = ["x", "fside_BxSxS_0", "itok_B_18_1004", "itok_B_0_2", "L0_cond_Wq", "L0_cond_bq", "L0_cond_Wk",
        "L0_cond_bk", "L0_cond_Wv", "L0_cond_bv", "L0_cond_Wo", "L0_cond_bo", "L0_cond_b_prev",
        "L0_cond_b_self", "L1_cond_W1", "L1_cond_b1", "L1_cond_v"]


def kernel(**inputs):
    import numpy as _np
    import concourse.bacc as _bacc
    from concourse.bass_utils import run_bass_kernel_spmd as _run

    nc = _bacc.Bacc("TRN2", target_bir_lowering=False, num_devices=1)
    arrays, args = {}, []
    for name in _INS:
        a = _np.ascontiguousarray(inputs[name])
        arrays[f"in_{name}"] = a
        args.append(nc.dram_tensor(f"in_{name}", a.shape, mybir.dt.from_np(a.dtype), kind="ExternalInput").ap())
    out = nc.dram_tensor("out_0", inputs["x"].shape, F32, kind="ExternalOutput").ap()
    build(nc, *args, out)
    return _run(nc, [arrays], core_ids=[0]).results[0]["out_0"]
```

```python
from contextlib import ExitStack

import concourse.bass as bass
from concourse import mybir

F32 = mybir.dt.float32
F32R = mybir.dt.float32r
I32 = mybir.dt.int32
ALU = mybir.AluOpType
ACT = mybir.ActivationFunctionType
AX = mybir.AxisListType

P = 128
MASKED = -1e30

SHARED = [
    ("TS", 1, 1, ("st_lo", 1)), ("PV0", -1, 2, ("pv_copied", 1)),
    ("MT1", -1, 0, ("mt_copied", 2)), ("AT", -2, 3, ("at_lo", 1)), ("TX", 1, 2, ("xt_lo", 1)),
    ("Q", 1, 0, ("q_copied", 1)),
    ("WO", -2, 1, ("x1_done", 1)),
    ("PV1", -1, 3, ("pv_copied", 2)),
    ("X1T", -2, 0, ("x1t_copied", 1)), ("K", 1, 2, ("k_copied", 1)),
    ("KS", 1, 1, ("prod_done", 1)),
    ("Z", -2, 0, ("tanh_done", 1)),
    ("PV2", -1, 3, ("pv_copied", 3)),
    ("MT0", 0, 0, ("mt_copied", 1)), ("SB", -2, 2, ("masked_done", 1)), ("VS", 1, 1, ("vs_copied", 1)),
    ("SS", 1, 0, ("ss_copied", 1)),
    ("V", 1, 2, ("v_copied", 1)),
    ("PV3", -1, 3, ("pv_copied", 4)), ("PT", -2, 0, ("pt_copied", 1)),
    ("NAT0", -1, 1, ("num_done", 1)), ("NAT1", -1, 0, ("num_done", 2)),
    ("PO", -2, 3, ("out_done", 1)),
]
BANKS = 4
PER_BATCH = {"mt_copied": 2, "num_done": 2, "pv_copied": 4}


def build(nc, x, side, seq_len, kind, Wq, bq, Wk, bk, Wv, bv, Wo, bo, b_prev, b_self, W1, b1, v, out):
    B, S, D = x.shape
    DH = 16
    H = D // DH
    NJ = H // 2
    KB = D // P
    A = W1.shape[1]
    ROWS = 3 * DH
    R_MASK, R_MAX = ROWS, ROWS + 1
    KM = ROWS + 1
    KF = ROWS + 3
    SLOTS = H
    LAG = 12
    GRP = 4
    NG = H // GRP
    MG = 8
    NM = H // MG
    MJ = MG // 2
    QSCALE = 1.0 / DH ** 0.5
    assert (S, D, H, KB, SLOTS) == (256, 256, 16, 2, 16)

    with ExitStack() as ctx:
        def sb(name, shape, dt=F32):
            return ctx.enter_context(nc.sbuf_tensor(name, shape, dt))

        def ps(name, shape):
            return ctx.enter_context(nc.psum_tensor(name, shape, F32))

        sems = {}

        def sem(name):
            sems[name] = ctx.enter_context(nc.semaphore(name))
            return sems[name]

        ps_max = ps("ps_max", [P, 2, KB, S])
        ps_exp = ps("ps_exp", [P, 2, KB, S])
        ps_any = ps("ps_any", [P, BANKS, KB, S])

        ident = sb("ident", [P, P])
        zeros = sb("zeros", [P, P])
        w_raw = sb("w_raw", [P, 4, KB, D])
        w_hi = sb("w_hi", [P, 4, KB, D], F32R)
        w_lo = sb("w_lo", [P, 4, KB, D], F32R)
        w1 = sb("w1", [P, KB, A])
        b1_col = sb("b1_col", [A, 1])
        v_col = sb("v_col", [A, 1])
        v_wide = sb("v_wide", [A, P])
        bqk_raw = sb("bqk_raw", [P, 2, 2])
        bqk_part = sb("bqk_part", [P, 3, 2])
        bqk_col = sb("bqk_col", [P, 3, 2])
        bin_col = sb("bin_col", [P, KB, 2])
        bv_wide = sb("bv_wide", [P, D])
        bo_wide = sb("bo_wide", [P, D])
        bin_parts = sb("bin_parts", [P, KB, 2, 2], F32R)
        headsum = sb("headsum", [P, NJ], F32R)
        len_i = sb("len_i", [B, 1], I32)
        len_f = sb("len_f", [B, 1])
        key_pos = sb("key_pos", [B, S])
        mask_row = sb("mask_row", [B, S], F32)
        kind_i = sb("kind_i", [P, B], I32)
        kind_f = sb("kind_f", [P, B])
        is0 = sb("is0", [P, B])
        is1 = sb("is1", [P, B])
        code = sb("code", [P, B])
        rowpos = sb("rowpos", [P, KB])
        side_of = sb("side_of", [P, KB, S])
        cnt = sb("cnt", [P, B, KB])
        cnt_a = sb("cnt_a", [P, KB])
        cnt_b = sb("cnt_b", [P, KB])

        x_sb = sb("x_sb", [P, 2, KB, D])
        s_sb = sb("s_sb", [P, 2, KB, D])
        xt_hi = sb("xt_hi", [P, KB, S], F32R)
        xt_lo = sb("xt_lo", [P, KB, S], F32R)
        st_hi = sb("st_hi", [P, KB, S], F32R)
        st_lo = sb("st_lo", [P, KB, S], F32R)
        q_full = sb("q_full", [P, 2, S])
        k_full = sb("k_full", [P, 2, S])
        q_hi = sb("q_hi", [P, 2, S], F32R)
        q_lo = sb("q_lo", [P, 2, S], F32R)
        k_hi = sb("k_hi", [P, 2, S], F32R)
        k_lo = sb("k_lo", [P, 2, S], F32R)
        prod = sb("prod", [P, 2, S])
        prod_hi = sb("prod_hi", [P, 2, S], F32R)
        prod_lo = sb("prod_lo", [P, 2, S], F32R)
        q_rows = [sb(f"q_rows{i}", [P, NJ, S], F32R) for i in range(2)]
        k_rows = [sb(f"k_rows{i}", [P, NJ, S], F32R) for i in range(2)]
        v_aug = [sb(f"v_aug{i}", [P, KB, H, 32]) for i in range(2)]
        v_self = sb("v_self", [P, 2, KB, D])
        s_self = sb("s_self", [P, 2, NM, KB, 2, MJ])
        s_max = sb("s_max", [P, NM, KB, 2, MJ])
        t_max = sb("t_max", [P, NM, KB, 2, MJ])
        neg_max = sb("neg_max", [P, NM, KB, 2, 2, MJ])
        mt_sb = sb("mt_sb", [4 * MJ, NM, S])
        p_arg = sb("p_arg", [P, KB, H])
        p_self = sb("p_self", [P, KB, H])
        pt = sb("pt", [P, 2 * GRP, KB, S])
        o_sb = sb("o_sb", [P, NG, S])
        vs_p = sb("vs_p", [P, KB, D])
        den = sb("den", [P, KB, H])
        rden = sb("rden", [P, KB, H])
        num = sb("num", [P, KB, D])
        attn = sb("attn", [P, KB, D])
        at_hi = sb("at_hi", [P, KB, S], F32R)
        at_lo = sb("at_lo", [P, KB, S], F32R)
        xr_sb = sb("xr_sb", [P, KB, D])
        x_bo = sb("x_bo", [P, KB, D])
        x1 = sb("x1", [P, KB, D])
        x1t = sb("x1t", [P, KB, S])
        z_sb = sb("z_sb", [A, S])
        hidden = sb("hidden", [P, KB, S])
        masked = sb("masked", [P, KB, S])
        row_max = sb("row_max", [P, KB])
        pool_p = sb("pool_p", [P, KB, S])
        pool_pt = sb("pool_pt", [P, KB, S])
        pool_sum = sb("pool_sum", [P, KB])
        pool_den = sb("pool_den", [P, KB])
        pool_r = sb("pool_r", [P, KB])
        o_out = sb("o_out", [P, KB, D])

        q_spill = nc.dram_tensor("q_spill", [2, 3, P, S], F32).ap()
        k_spill = nc.dram_tensor("k_spill", [2, 3, P, S], F32).ap()
        mask_dram = nc.dram_tensor("mask_dram", [B, S], F32).ap()

        consts_loaded = sem("consts_loaded")
        bias_loaded = sem("bias_loaded")
        lens_loaded = sem("lens_loaded")
        weights_loaded = [sem(f"weights_loaded{n}") for n in range(4)]
        pool_zero = sem("pool_zero")
        ident_ready = sem("ident_ready")
        pool_const = sem("pool_const")
        masks_ready = sem("masks_ready")
        masks_stored = sem("masks_stored")
        dve_const = sem("dve_const")
        len_ready, code_ready, v_wide_ready = sem("len_ready"), sem("code_ready"), sem("v_wide_ready")
        w_hi_ready = sem("w_hi_ready")
        w_lo_ready = sem("w_lo_ready")
        bias_ready = sem("bias_ready")
        bias_copied = sem("bias_copied")
        rows_one = sem("rows_one")
        v_zeroed = sem("v_zeroed")
        bias_scaled = sem("bias_scaled")
        bin_hi_done, bin_lo_done, bias_part_done = sem("bin_hi_done"), sem("bin_lo_done"), sem("bias_part_done")
        headsum_ready = sem("headsum_ready")
        x_loaded = [sem(f"x_loaded{i}") for i in range(2)]
        s_loaded = [sem(f"s_loaded{i}") for i in range(2)]
        xr_loaded = sem("xr_loaded")
        xt_ready, xt_hi_done, xt_lo_done = sem("xt_ready"), sem("xt_hi_done"), sem("xt_lo")
        st_ready, st_hi_done, st_lo_done = sem("st_ready"), sem("st_hi_done"), sem("st_lo")
        q_ready, q_full_done, q_copied, q_lo_done = sem("q_ready"), sem("q_full_done"), sem("q_copied"), sem("q_lo_done")
        k_ready, k_full_done, k_copied, k_lo_done = sem("k_ready"), sem("k_full_done"), sem("k_copied"), sem("k_lo_done")
        q_spilled, k_spilled = sem("q_spilled"), sem("k_spilled")
        q_placed, k_placed = ([sem(f"{name}_placed{g}") for g in range(NM)] for name in "qk")
        prod_hi_done, prod_lo_done = sem("prod_hi_done"), sem("prod_lo_done")
        ks_ready, prod_done, ss_ready, ss_copied = sem("ks_ready"), sem("prod_done"), sem("ss_ready"), sem("ss_copied")
        v_ready, v_copied, vs_ready, vs_copied = sem("v_ready"), sem("v_copied"), sem("vs_ready"), sem("vs_copied")
        max_scored, max_found = sem("max_scored"), sem("max_found")
        total_max, neg_hi, neg_done = sem("total_max"), sem("neg_hi"), sem("neg_done")
        mt_ready, mt_copied = sem("mt_ready"), sem("mt_copied")
        max_placed = [sem(f"max_placed{g}") for g in range(NM)]
        p_arg_done, p_self_done = sem("p_arg_done"), sem("p_self_done")
        scored, p_ready, pv_ready, pv_copied = sem("scored"), sem("p_ready"), sem("pv_ready"), sem("pv_copied")
        vs_p_done, nat_ready = sem("vs_p_done"), sem("nat_ready")
        den_done, rden_done, num_done, attn_done = sem("den_done"), sem("rden_done"), sem("num_done"), sem("attn_done")
        at_ready, at_hi_done, at_lo_done = sem("at_ready"), sem("at_hi_done"), sem("at_lo")
        wo_ready, x_bo_done, x1_done = sem("wo_ready"), sem("x_bo_done"), sem("x1_done")
        x1t_ready, x1t_copied, z_ready, tanh_done = sem("x1t_ready"), sem("x1t_copied"), sem("z_ready"), sem("tanh_done")
        sb_ready, hidden_done, masked_done, row_max_done = sem("sb_ready"), sem("hidden_done"), sem("masked_done"), sem("row_max_done")
        pool_p_done, pt_ready, pt_copied = sem("pool_p_done"), sem("pt_ready"), sem("pt_copied")
        po_ready, pool_den_done, pool_r_done, out_done, out_stored = (
            sem("po_ready"), sem("pool_den_done"), sem("pool_r_done"), sem("out_done"), sem("out_stored"))

        def live(i, k):
            return not isinstance(i, int) or 0 <= 2 * i + k < B

        def count(i, k, per, done):
            n = i * (2 * per) + (k * per + done)
            return n if not isinstance(i, int) or n > 0 else None

        def row(dram, i, k):
            names = " ".join("abc"[:len(dram.shape) - 1])
            return dram.rearrange(f"(i k) {names} -> i k {names}", k=2)[i + k // 2, k % 2]

        def bank_free(step, i, k):
            at, bank = next((n, entry[2]) for n, entry in enumerate(SHARED) if entry[0] == step)
            for back in range(at - 1, -2 * len(SHARED), -1):
                name, offset, used, (reader, done) = SHARED[back % len(SHARED)]
                kk = k + back // len(SHARED) + offset
                if used == bank and live(i, kk):
                    return bank, sems[reader], count(i, kk, PER_BATCH.get(reader, 1), done)
            return bank, None, None

        PERIODS = [(n // 2, n % 2) for n in range(-1, B + 2)]
        LOOP_FROM, LOOP_TO = 1, 3
        BEFORE, BODY, AFTER = PERIODS[:4], (1, 2), PERIODS[8:]

        x_rows = x.rearrange("b (t p) d -> b p t d", p=P)
        s_rows = side.rearrange("b (t p) d -> b p t d", p=P)
        out_rows = out.rearrange("b (t p) d -> b p t d", p=P)

        block = ctx.enter_context(nc.Block())

        @block.sync
        def _(sp):
            def load(i, k):
                if live(i, k):
                    par = k % 2
                    if (n := count(i, k, 1, -1)) is not None:
                        sp.wait_ge(xt_ready, n)
                    sp.dma_start(x_sb[:, par], row(x_rows, i, k)).then_inc(x_loaded[par], 16)
                    if (n := count(i, k, 1, -1)) is not None:
                        sp.wait_ge(st_ready, n)
                    sp.dma_start(s_sb[:, par], row(s_rows, i, k)).then_inc(s_loaded[par], 16)

            def store(i, k):
                if live(i, k):
                    sp.wait_ge(out_done, count(i, k, 1, 1))
                    sp.dma_start(row(out_rows, i, k), o_out[:]).then_inc(out_stored, 16)

            def spill(i, k, hi, lo, lo_done, pattern, dram, placed, placed_per, spilled):
                n_lo = held(count(i, k, 1, 1))
                if (n := held(count(i, k, placed_per, 0))) is not None:
                    for half in placed:
                        sp.wait_ge(half, n)
                sp.wait_ge(lo_done, n_lo)
                for c, part in enumerate(pattern):
                    src = (hi, lo)[part][:].bitcast(F32)
                    sp.dma_start(dram[:, c].rearrange("e p t -> p e t"), src).then_inc(spilled, 16)

            def held(n):
                return n if n is None or isinstance(n, int) else sp.to_reg(n)

            def place(dram, rows, placed, g):
                for e in range(2):
                    sp.dma_start(rows[64 * e:64 * e + ROWS, MJ * g:MJ * g + MJ].bitcast(F32),
                                 dram[e].rearrange("c (d j) t -> (c d) j t", d=DH)[:, MJ * g:MJ * g + MJ]
                                 ).then_inc(placed[g], 16)

            def place_max(i, k, g):
                par = k % 2
                sp.wait_ge(mt_copied, count(i, k, NM, g + 1))
                for e in range(2):
                    sp.dma_start(q_rows[par][64 * e + R_MAX:64 * e + R_MAX + 2, MJ * g:MJ * g + MJ, :].bitcast(F32),
                                 mt_sb[2 * MJ * e:2 * MJ * e + 2 * MJ, g, :]).then_inc(max_placed[g], 16)

            def period(i, k):
                b, nxt, prv = (i, k), (i, k + 1), (i, k - 1)
                if not isinstance(i, int) or 2 * i + k >= 1:
                    load(*nxt)
                if live(*prv):
                    place_max(*prv, 1)
                store(i, k - 3)
                if live(*nxt):
                    spill(*nxt, q_hi, q_lo, q_lo_done, (0, 0, 1), q_spill, q_placed, 32, q_spilled)
                    spill(*nxt, k_hi, k_lo, k_lo_done, (0, 1, 0), k_spill, k_placed, 48, k_spilled)
                if live(*b):
                    place_max(*b, 0)
                if live(*nxt):
                    par = (k + 1) % 2
                    mask = row(mask_dram, *nxt).unsqueeze(0).unsqueeze(0).broadcast_to([2, MJ, S])
                    n_spilled = held(count(*nxt, 48, 48))
                    n_scored = [held(count(*nxt, H, MG * (g + 1) - 2 * H)) for g in range(NM)]
                    for g in range(NM):
                        if n_scored[g] is not None:
                            sp.wait_ge(scored, n_scored[g])
                        elif g == 0:
                            sp.wait_ge(rows_one, par + 1)
                        if g == 0:
                            sp.wait_ge(q_spilled, n_spilled)
                        place(q_spill, q_rows[par], q_placed, g)
                        if g == 0:
                            sp.wait_ge(k_spilled, n_spilled)
                            if isinstance(i, int):
                                sp.wait_ge(masks_stored, 16)
                        place(k_spill, k_rows[par], k_placed, g)
                        sp.dma_start(k_rows[par][R_MASK:R_MASK + 65:64, MJ * g:MJ * g + MJ].bitcast(F32), mask
                                     ).then_inc(k_placed[g], 16)
                if live(*prv):
                    if (n := count(*prv, 1, 0)) is not None:
                        sp.wait_ge(x_bo_done, n)
                    sp.dma_start(xr_sb[:], row(x_rows, *prv)).then_inc(xr_loaded, 16)

            def load_weight(n):
                sp.dma_start(w_raw[:, n], (Wq, Wk, Wv, Wo)[n].rearrange("(k p) n -> p k n", p=P)
                             ).then_inc(weights_loaded[n], 16)

            sp.dma_start(s_sb[:, 0], s_rows[0]).then_inc(s_loaded[0], 16)
            load_weight(0)
            sp.dma_start(x_sb[:, 0], x_rows[0]).then_inc(x_loaded[0], 16)
            load_weight(1)
            with nc.allow_non_contiguous_dma("bias vectors, once"):
                for n, vec in enumerate((b_self, b_prev)):
                    sp.dma_start(bin_col[:, :, n], vec.rearrange("a b (k p) -> p (a b k)", p=P)
                                 ).then_inc(bias_loaded, 16)
                for n, vec in enumerate((bq, bk)):
                    sp.dma_start(bqk_raw[:, n, :], vec.rearrange("(j e d) -> d j e", e=2, d=DH)
                                 ).then_inc(bias_loaded, 16)
            sp.dma_start(len_i[:], seq_len.unsqueeze(1)).then_inc(lens_loaded, 16)
            load_weight(2)
            sp.dma_start(bv_wide[:], bv.partition_broadcast(P)).then_inc(consts_loaded, 16)
            sp.dma_start(kind_i[:], kind.partition_broadcast(P)).then_inc(consts_loaded, 16)
            sp.dma_start(bo_wide[:], bo.partition_broadcast(P)).then_inc(consts_loaded, 16)
            sp.dma_start(w1[:], W1.rearrange("(k p) a -> p k a", p=P)).then_inc(consts_loaded, 16)
            sp.dma_start(b1_col[:], b1.unsqueeze(1)).then_inc(consts_loaded, 16)
            sp.dma_start(v_col[:], v.unsqueeze(1)).then_inc(consts_loaded, 16)
            load_weight(3)
            load(0, 1)
            sp.wait_ge(masks_ready, 1)
            sp.dma_start(mask_dram, mask_row[:]).then_inc(masks_stored, 16)

            for i, k in BEFORE:
                period(i, k)
            with sp.Fori(LOOP_FROM, LOOP_TO) as i:
                for k in BODY:
                    period(i, k)
            for i, k in AFTER:
                period(i, k)
            store(B // 2 - 1, 1)
            sp.wait_ge(out_stored, 16 * B)

        @block.gpsimd
        def _(pool):
            def ones_rows(par):
                nc.gpsimd.memset(q_rows[par][:].bitcast(F32), 1.0)
                nc.gpsimd.memset(k_rows[par][:].bitcast(F32), 1.0).then_inc(rows_one, 1)

            nc.gpsimd.memset(ident[:], 0.0).then_inc(pool_zero, 1)
            nc.gpsimd.memset(side_of[:], 0.0).then_inc(pool_zero, 1)
            pool.wait_ge(pool_zero, 1)
            nc.gpsimd.affine_select(out=ident[:], in_=ident[:], compare_op=ALU.not_equal, fill=1.0, base=0,
                                    pattern=[[-1, P]], channel_multiplier=1).then_inc(ident_ready, 1)
            nc.gpsimd.iota(key_pos[:], pattern=[[1, S]], base=0, channel_multiplier=0,
                           allow_small_or_imprecise_dtypes=True).then_inc(pool_const, 1)
            ones_rows(0)
            nc.gpsimd.iota(rowpos[:], pattern=[[P, KB]], base=0, channel_multiplier=1,
                           allow_small_or_imprecise_dtypes=True).then_inc(pool_const, 1)
            pool.wait_ge(pool_zero, 2)
            nc.gpsimd.affine_select(out=side_of[:], in_=side_of[:], compare_op=ALU.is_ge, fill=1.0, base=0,
                                    pattern=[[P, KB], [-1, S]], channel_multiplier=1).then_inc(pool_const, 1)
            pool.wait_ge(pool_const, 3)
            nc.gpsimd.affine_select(out=side_of[:], in_=side_of[:], compare_op=ALU.is_ge, fill=-1.0, base=0,
                                    pattern=[[-P, KB], [1, S]], channel_multiplier=-1).then_inc(pool_const, 1)

            def split_lo(i, k, full_done, hi_done, full, hi, lo, lo_done, spilled):
                pool.wait_ge(full_done, count(i, k, 1, 1))
                pool.wait_ge(hi_done, count(i, k, 1, 1))
                if (n := count(i, k, 48, 0)) is not None:
                    pool.wait_ge(spilled, n)
                nc.gpsimd.tensor_tensor(lo[:], full[:], hi[:].bitcast(F32), ALU.subtract).then_inc(lo_done, 1)

            def period(i, k):
                b, nxt, prv = (i, k), (i, k + 1), (i, k - 1)
                if live(*prv):
                    par = (k - 1) % 2
                    pool.wait_ge(p_self_done, count(*prv, 1, 1))
                    pool.wait_ge(vs_copied, count(*prv, 1, 1))
                    if (n := count(*prv, 2, 0)) is not None:
                        pool.wait_ge(num_done, n)
                    for t in range(KB):
                        last = nc.gpsimd.tensor_tensor(
                            vs_p[:, t].rearrange("p (h d) -> p h d", d=DH),
                            v_self[:, par, t].rearrange("p (h d) -> p h d", d=DH),
                            p_self[:, t].unsqueeze(2).broadcast_to([P, H, DH]), ALU.mult)
                    last.then_inc(vs_p_done, 1)
                if live(*nxt):
                    split_lo(*nxt, q_full_done, q_copied, q_full, q_hi, q_lo, q_lo_done, q_spilled)
                    split_lo(*nxt, k_full_done, k_copied, k_full, k_hi, k_lo, k_lo_done, k_spilled)
                    pool.wait_ge(prod_hi_done, count(*nxt, 1, 1))
                    if (n := count(*nxt, 1, 0)) is not None:
                        pool.wait_ge(ss_ready, n)
                    nc.gpsimd.tensor_tensor(prod_lo[:], prod[:], prod_hi[:].bitcast(F32), ALU.subtract
                                            ).then_inc(prod_lo_done, 1)
                if isinstance(i, int) and i < 0:
                    ones_rows(1)
                if live(*prv):
                    if (n := count(*prv, 1, 0)) is not None:
                        pool.wait_ge(at_ready, n)
                    for t in range(KB):
                        pool.wait_ge(num_done, count(*prv, 2, t + 1))
                        nc.gpsimd.tensor_tensor(
                            attn[:, t].rearrange("p (h d) -> p h d", d=DH),
                            num[:, t].rearrange("p (h d) -> p h d", d=DH),
                            rden[:, t].unsqueeze(2).broadcast_to([P, H, DH]), ALU.mult).then_inc(attn_done, 1)
                    pool.wait_ge(xr_loaded, count(*prv, 16, 16))
                    if (n := count(*prv, 1, 0)) is not None:
                        pool.wait_ge(x1_done, n)
                    nc.gpsimd.tensor_tensor(x_bo[:], xr_sb[:], bo_wide[:].unsqueeze(1).broadcast_to([P, KB, D]),
                                            ALU.add).then_inc(x_bo_done, 1)

            for i, k in BEFORE:
                period(i, k)
            with pool.Fori(LOOP_FROM, LOOP_TO) as i:
                for k in BODY:
                    period(i, k)
            for i, k in AFTER:
                period(i, k)

        @block.scalar
        def _(act):
            def max_rows_copy(i, k, g, pi, pk):
                act.wait_ge(mt_ready, count(i, k, NM, g + 1))
                if (n := count(i, k, 32, 0)) is not None:
                    act.wait_ge(max_placed[g], n)
                nc.scalar.activation(mt_sb[:, g, :], ps_any[0:4 * MJ, bank_free(f"MT{g}", pi, pk)[0], 0, :],
                                     ACT.Copy).then_inc(mt_copied, 1)

            def exps(i, k, h):
                act.wait_ge(scored, count(i, k, H, h + 1))
                if (n := count(i, k, NG, h // GRP - 1)) is not None:
                    act.wait_ge(pv_ready, n)
                nc.scalar.activation(pt[:, h % 8], ps_exp[:, h % 2], ACT.Exp).then_inc(p_ready, 1)

            def pv_copy(i, k, g):
                act.wait_ge(pv_ready, count(i, k, NG, g + 1))
                if (n := count(i, k, 2, 0)) is not None:
                    act.wait_ge(nat_ready, n)
                nc.scalar.activation(o_sb[:, g], ps_any[:, bank_free(f"PV{g}", i, k)[0], 0, :], ACT.Copy).then_inc(pv_copied, 1)

            def weight_hi(n):
                act.wait_ge(weights_loaded[n], 16)
                for kb in range(KB):
                    dst, src = w_hi[:, n, kb], w_raw[:, n, kb]
                    if n < 2:
                        dst = dst.rearrange("p (e d j) -> p e d j", e=2, d=DH)
                        src = src.rearrange("p (j e d) -> p e d j", e=2, d=DH)
                    nc.scalar.activation(dst, src, ACT.Copy, scale=QSCALE if n == 0 else 1.0
                                         ).then_inc(w_hi_ready, 1)

            def period(i, k):
                b, nxt, prv, old = (i, k), (i, k + 1), (i, k - 1), (i, k - 2)
                first = isinstance(i, int) and i < 0
                for s in range(SLOTS):
                    if s == 1 and live(*nxt):
                        act.wait_ge(st_ready, count(*nxt, 1, 1))
                        if (n := count(*nxt, 1, 0)) is not None:
                            act.wait_ge(vs_ready, n)
                        nc.scalar.activation(st_hi[:], ps_any[:, bank_free("TS", i, k)[0]], ACT.Copy
                                             ).then_inc(st_hi_done, 1)
                        if first:
                            weight_hi(1)
                    g = {1: 0, 5: 1, 9: 2, 13: 3}.get(s)
                    if g is not None and live(*prv):
                        pv_copy(*prv, g)
                    if s == 1 and live(*prv):
                        max_rows_copy(*prv, 1, i, k)
                    if s == 9 and live(*b):
                        max_rows_copy(*b, 0, i, k)
                    if s == 2:
                        if live(*old):
                            act.wait_ge(at_ready, count(*old, 1, 1))
                            if (n := count(*old, 1, 0)) is not None:
                                act.wait_ge(wo_ready, n)
                            nc.scalar.activation(at_hi[:], ps_any[:, bank_free("AT", i, k)[0]], ACT.Copy
                                                 ).then_inc(at_hi_done, 1)
                        if live(*nxt):
                            act.wait_ge(xt_ready, count(*nxt, 1, 1))
                            if (n := count(*nxt, 1, 0)) is not None:
                                act.wait_ge(v_ready, n)
                            nc.scalar.activation(xt_hi[:], ps_any[:, bank_free("TX", i, k)[0]], ACT.Copy
                                                 ).then_inc(xt_hi_done, 1)
                        if first:
                            weight_hi(2)
                    if s == 3 and live(*nxt):
                        qk_copy(*nxt, "Q", i, k)
                    if s == 4 and live(*prv):
                        act.wait_ge(p_arg_done, count(*prv, 1, 1))
                        if (n := count(*prv, 1, 0)) is not None:
                            act.wait_ge(vs_p_done, n)
                            act.wait_ge(den_done, count(*prv, 2, 0))
                        nc.scalar.activation(p_self[:], p_arg[:], ACT.Exp).then_inc(p_self_done, 1)
                    if s == 6 and live(*old):
                        act.wait_ge(x1t_ready, count(*old, 1, 1))
                        if (n := count(*old, 1, 0)) is not None:
                            act.wait_ge(z_ready, n)
                        nc.scalar.activation(x1t[:], ps_any[:, bank_free("X1T", i, k)[0]], ACT.Copy
                                             ).then_inc(x1t_copied, 1)
                    if s == 7 and live(*nxt):
                        qk_copy(*nxt, "K", i, k)
                        if first:
                            weight_hi(3)
                    if s == 8 and live(*old):
                        act.wait_ge(z_ready, count(*old, 1, 1))
                        if (n := count(*old, 1, 0)) is not None:
                            act.wait_ge(sb_ready, n)
                        nc.scalar.activation(z_sb[:], ps_any[0:A, bank_free("Z", i, k)[0], 0, :], ACT.Tanh,
                                             bias=b1_col[:, 0:1]).then_inc(tanh_done, 1)
                    if s == 11 and live(*nxt):
                        par = (k + 1) % 2
                        act.wait_ge(ss_ready, count(*nxt, 1, 1))
                        if (n := count(*nxt, 1, -1)) is not None:
                            act.wait_ge(p_arg_done, n)
                        nc.scalar.activation(s_self[:, par].rearrange("p g t e j -> p (g t e j)"),
                                             ps_any[:, bank_free("SS", i, k)[0], 0, 0:2 * H], ACT.Copy
                                             ).then_inc(ss_copied, 1)
                    if s == 11 and live(*old):
                        act.wait_ge(row_max_done, count(*old, 1, 1))
                        if (n := count(*old, 1, 0)) is not None:
                            act.wait_ge(pt_ready, n)
                            act.wait_ge(pool_den_done, n)
                        for t in range(KB):
                            nc.scalar.activation(pool_p[:, t], masked[:, t], ACT.Exp,
                                                 bias=row_max[:, t:t + 1], accum_out=pool_sum[:, t:t + 1]
                                                 ).then_inc(pool_p_done, 1)
                    if s == 13 and live(*old):
                        act.wait_ge(pt_ready, count(*old, 1, 1))
                        if (n := count(*old, 1, 0)) is not None:
                            act.wait_ge(po_ready, n)
                        nc.scalar.activation(pool_pt[:], ps_any[:, bank_free("PT", i, k)[0]], ACT.Copy
                                             ).then_inc(pt_copied, 1)
                    who = b if s >= LAG else prv
                    if live(*who):
                        exps(*who, (s - LAG) % SLOTS)

            def qk_copy(i, k, step, pi, pk):
                ready, full, hi, full_done, hi_done, lo_done, spilled, n_bias = {
                    "Q": (q_ready, q_full, q_hi, q_full_done, q_copied, q_lo_done, q_spilled, 0),
                    "K": (k_ready, k_full, k_hi, k_full_done, k_copied, k_lo_done, k_spilled, 1)}[step]
                bank = bank_free(step, pi, pk)[0]
                act.wait_ge(ready, count(i, k, 1, 1))
                if (n := count(i, k, 1, 0)) is not None:
                    act.wait_ge(lo_done, n)
                    if step == "Q":
                        act.wait_ge(prod_done, n)
                else:
                    act.wait_ge(bias_copied, 1)
                for m in range(2):
                    last = nc.scalar.activation(full[:, m], ps_any[:, bank, m], ACT.Identity,
                                                bias=bqk_col[:, n_bias, m:m + 1])
                last.then_inc(full_done, 1)
                if (n := count(i, k, 48, 0)) is not None:
                    act.wait_ge(spilled, n)
                for m in range(2):
                    last = nc.scalar.activation(hi[:, m], ps_any[:, bank, m], ACT.Identity,
                                                bias=bqk_col[:, n_bias, m:m + 1])
                last.then_inc(hi_done, 1)

            weight_hi(0)
            for i, k in BEFORE:
                period(i, k)
            with act.Fori(LOOP_FROM, LOOP_TO) as i:
                for k in BODY:
                    period(i, k)
            for i, k in AFTER:
                period(i, k)

        @block.vector
        def _(dve):
            def weight_lo(n):
                for kb in range(KB):
                    dve.wait_ge(w_hi_ready, KB * n + kb + 1)
                    if n < 2:
                        for e in range(2):
                            hi, lo = (w[:, n, kb].rearrange("p (e d j) -> p e d j", e=2, d=DH)[:, e]
                                      for w in (w_hi, w_lo))
                            src = w_raw[:, n, kb].rearrange("p (j e d) -> p e d j", e=2, d=DH)[:, e]
                            last = nc.vector.scalar_tensor_tensor(
                                out=lo, in0=src, scalar=QSCALE if n == 0 else 1.0,
                                in1=hi.bitcast(F32), op0=ALU.mult, op1=ALU.subtract)
                    else:
                        last = nc.vector.tensor_tensor(w_lo[:, n, kb], w_raw[:, n, kb],
                                                       w_hi[:, n, kb].bitcast(F32), ALU.subtract)
                last.then_inc(w_lo_ready, 1)

            def split_bias_inputs():
                dve.wait_ge(bias_loaded, 4 * 16)
                nc.vector.tensor_copy(bin_parts[:, :, 0], bin_col[:]).then_inc(bin_hi_done, 1)
                nc.vector.tensor_scalar(bqk_raw[:, 0], bqk_raw[:, 0], QSCALE, None, ALU.mult
                                        ).then_inc(bias_scaled, 1)
                dve.wait_ge(bin_hi_done, 1)
                nc.vector.tensor_tensor(bin_parts[:, :, 1], bin_col[:], bin_parts[:, :, 0].bitcast(F32), ALU.subtract
                                        ).then_inc(bin_lo_done, 1)

            def setup_biases():
                dve.wait_ge(bias_scaled, 1)
                dve.wait_ge(bias_ready, 1)
                sums = ps_max[:, 0, 0, 0:16].rearrange("p (w m part c) -> p part w m c", w=2, m=2, part=2)
                cases = ((0, 0), (1, 1), (1, 0))
                for n, (w, c) in enumerate(cases):
                    last = nc.vector.tensor_tensor(bqk_part[:, n], sums[:, 0, w, :, c], bqk_raw[:, w], ALU.add)
                last.then_inc(bias_part_done, 1)
                dve.wait_ge(bias_part_done, 1)
                for n, (w, c) in enumerate(cases):
                    last = nc.vector.tensor_tensor(bqk_col[:, n], sums[:, 1, w, :, c], bqk_part[:, n], ALU.add)
                last.then_inc(bias_copied, 1)

            def setup_masks():
                dve.wait_ge(lens_loaded, 16)
                nc.vector.tensor_copy(len_f[:], len_i[:]).then_inc(len_ready, 1)
                dve.wait_ge(len_ready, 1)
                dve.wait_ge(pool_const, 4)
                nc.vector.tensor_scalar(mask_row[:], key_pos[:], len_f[:, 0:1], MASKED, ALU.is_ge, ALU.mult
                                        ).then_inc(masks_ready, 1)

            def setup_v():
                for par in range(2):
                    last = nc.vector.memset(v_aug[par][:], 0.0)
                last.then_inc(v_zeroed, 1)
                dve.wait_ge(v_zeroed, 1)
                for par in range(2):
                    nc.vector.memset(v_aug[par][:, :, :, DH:DH + 1], 1.0)
                dve.wait_ge(consts_loaded, 6 * 16)

            def setup_pooling():
                nc.vector.memset(zeros[:], 0.0).then_inc(dve_const, 1)
                nc.vector.tensor_copy(kind_f[:], kind_i[:]).then_inc(dve_const, 1)
                nc.vector.tensor_scalar(cnt_a[:], rowpos[:], float(2 - S), None, ALU.add).then_inc(dve_const, 1)
                nc.vector.tensor_scalar(cnt_b[:], rowpos[:], -1.0, 1.0, ALU.mult, ALU.add).then_inc(dve_const, 1)
                nc.vector.memset(cnt[:], float(S - 1)).then_inc(dve_const, 1)
                dve.wait_ge(dve_const, 5)
                nc.vector.tensor_scalar(v_wide[:], zeros[0:A, :], v_col[:, 0:1], None, ALU.add
                                        ).then_inc(v_wide_ready, 1)
                nc.vector.tensor_scalar(is0[:], kind_f[:], 0.0, None, ALU.is_equal).then_inc(dve_const, 1)
                nc.vector.tensor_scalar(is1[:], kind_f[:], 1.0, None, ALU.is_equal).then_inc(dve_const, 1)
                n_const = 7
                dve.wait_ge(dve_const, n_const)
                nc.vector.tensor_tensor(code[:], is0[:], is1[:], ALU.subtract).then_inc(code_ready, 1)
                for sel, diff in ((is0, cnt_a), (is1, cnt_b)):
                    for t in range(KB):
                        nc.vector.scalar_tensor_tensor(out=cnt[:, :, t], in0=sel[:], scalar=diff[:, t:t + 1],
                                                       in1=cnt[:, :, t], op0=ALU.mult, op1=ALU.add
                                                       ).then_inc(dve_const, 1)
                    n_const += KB
                    dve.wait_ge(dve_const, n_const)

            def max_of(i, k, h):
                dve.wait_ge(max_scored, count(i, k, H, h + 1))
                nc.vector.tensor_reduce(s_max[:, h // MG, :, h % 2, h // 2 % MJ], ps_max[:, h % 2], AX.X, ALU.max
                                        ).then_inc(max_found, 1)

            def group_max(i, k, g):
                dve.wait_ge(max_found, count(i, k, H, MG * (g + 1)))
                dve.wait_ge(ss_copied, count(i, k, 1, 1))
                nc.vector.tensor_tensor(t_max[:, g], s_max[:, g], s_self[:, k % 2, g], ALU.max
                                        ).then_inc(total_max, 1)
                dve.wait_ge(total_max, count(i, k, NM, g + 1))
                if (n := count(i, k, NM, g + 1 - NM)) is not None:
                    dve.wait_ge(mt_ready, n)
                nc.vector.tensor_scalar(neg_max[:, g, :, :, 0].bitcast(F32R), t_max[:, g], -1.0, None, ALU.mult
                                        ).then_inc(neg_hi, 1)
                dve.wait_ge(neg_hi, count(i, k, NM, g + 1))
                nc.vector.scalar_tensor_tensor(out=neg_max[:, g, :, :, 1].bitcast(F32R), in0=t_max[:, g],
                                               scalar=-1.0, in1=neg_max[:, g, :, :, 0],
                                               op0=ALU.mult, op1=ALU.subtract).then_inc(neg_done, 1)

            def period(i, k):
                b, nxt, prv, old = (i, k), (i, k + 1), (i, k - 1), (i, k - 2)
                first = isinstance(i, int) and i < 0
                for s in range(SLOTS):
                    if s == 1:
                        if live(*nxt):
                            dve.wait_ge(st_hi_done, count(*nxt, 1, 1))
                            nc.vector.tensor_tensor(st_lo[:], ps_any[:, bank_free("TS", i, k)[0]],
                                                    st_hi[:].bitcast(F32), ALU.subtract).then_inc(st_lo_done, 1)
                        if first:
                            split_bias_inputs()
                            weight_lo(1)
                    if s == 2:
                        if live(*old):
                            dve.wait_ge(at_hi_done, count(*old, 1, 1))
                            nc.vector.tensor_tensor(at_lo[:], ps_any[:, bank_free("AT", i, k)[0]],
                                                    at_hi[:].bitcast(F32), ALU.subtract).then_inc(at_lo_done, 1)
                        if live(*prv):
                            if (n := count(*prv, 1, 0)) is not None:
                                dve.wait_ge(p_self_done, n)
                            for t in range(KB):
                                for g in range(NM):
                                    last = nc.vector.tensor_tensor(
                                        p_arg[:, t, MG * g:MG * g + MG].rearrange("p (j e) -> p e j", e=2),
                                        s_self[:, (k - 1) % 2, g, t], t_max[:, g, t], ALU.subtract)
                            last.then_inc(p_arg_done, 1)
                    if s == 3:
                        if live(*nxt):
                            dve.wait_ge(xt_hi_done, count(*nxt, 1, 1))
                            nc.vector.tensor_tensor(xt_lo[:], ps_any[:, bank_free("TX", i, k)[0]],
                                                    xt_hi[:].bitcast(F32), ALU.subtract).then_inc(xt_lo_done, 1)
                        if first:
                            setup_biases()
                            setup_masks()
                            nc.vector.tensor_reduce(headsum[:], ident[:].rearrange("p (d j) -> p j d", j=NJ),
                                                    AX.X, ALU.max).then_inc(headsum_ready, 1)
                            weight_lo(2)
                    if s == 4 and live(*old):
                        dve.wait_ge(wo_ready, count(*old, 1, 1))
                        dve.wait_ge(x_bo_done, count(*old, 1, 1))
                        if (n := count(*old, 1, 0)) is not None:
                            dve.wait_ge(out_done, n)
                        nc.vector.tensor_tensor(x1[:], ps_any[:, bank_free("WO", i, k)[0]], x_bo[:], ALU.add
                                                ).then_inc(x1_done, 1)
                    if s == 6 and live(*old):
                        kk = k - 2
                        codes = code[:].rearrange("p (i k) -> p i k", k=2)
                        if (n := count(*old, 1, 0)) is not None:
                            dve.wait_ge(masked_done, n)
                        else:
                            dve.wait_ge(code_ready, 1)
                        nc.vector.tensor_scalar(hidden[:], side_of[:],
                                                codes[:, i + kk // 2, kk % 2:kk % 2 + 1],
                                                MASKED, ALU.is_equal, ALU.mult).then_inc(hidden_done, 1)
                    if s == 8 and live(*b):
                        group_max(*b, 0)
                    if s == 8 and live(*nxt):
                        dve.wait_ge(ks_ready, count(*nxt, 1, 1))
                        dve.wait_ge(q_full_done, count(*nxt, 1, 1))
                        if (n := count(*nxt, 1, 0)) is not None:
                            dve.wait_ge(prod_lo_done, n)
                        for m in range(2):
                            last = nc.vector.scalar_tensor_tensor(
                                out=prod[:, m], in0=ps_any[:, bank_free("KS", i, k)[0], m],
                                scalar=bqk_col[:, 2, m:m + 1], in1=q_full[:, m], op0=ALU.add, op1=ALU.mult)
                        last.then_inc(prod_done, 1)
                        dve.wait_ge(prod_done, count(*nxt, 1, 1))
                        if (n := count(*nxt, 1, 0)) is not None:
                            dve.wait_ge(ss_ready, n)
                        nc.vector.tensor_copy(prod_hi[:], prod[:]).then_inc(prod_hi_done, 1)
                        if first:
                            setup_v()
                    if s == 10 and live(*old):
                        dve.wait_ge(sb_ready, count(*old, 1, 1))
                        dve.wait_ge(hidden_done, count(*old, 1, 1))
                        if (n := count(*old, 2, 0)) is not None:
                            dve.wait_ge(pool_p_done, n)
                        nc.vector.tensor_tensor(
                            masked[:], hidden[:],
                            ps_any[:, bank_free("SB", i, k)[0], 0].unsqueeze(1).broadcast_to([P, KB, S]),
                            ALU.add).then_inc(masked_done, 1)
                        dve.wait_ge(masked_done, count(*old, 1, 1))
                        nc.vector.tensor_reduce(row_max[:], masked[:], AX.X, ALU.max, negate=True
                                                ).then_inc(row_max_done, 1)
                    if s == 11 and live(*nxt):
                        dve.wait_ge(vs_ready, count(*nxt, 1, 1))
                        if (n := count(*nxt, 1, -1)) is not None:
                            dve.wait_ge(vs_p_done, n)
                        nc.vector.tensor_tensor(v_self[:, (k + 1) % 2], ps_any[:, bank_free("VS", i, k)[0]],
                                                bv_wide[:].unsqueeze(1).broadcast_to([P, KB, D]), ALU.add
                                                ).then_inc(vs_copied, 1)
                    if s == 14 and live(*nxt):
                        dve.wait_ge(v_ready, count(*nxt, 1, 1))
                        if (n := count(*nxt, NG, -NG)) is not None:
                            dve.wait_ge(pv_ready, n)
                        for t in range(KB):
                            last = nc.vector.tensor_tensor(
                                v_aug[(k + 1) % 2][:, t, :, 0:DH],
                                ps_any[:, bank_free("V", i, k)[0], t].rearrange("p (h d) -> p h d", d=DH),
                                bv_wide[:].rearrange("p (h d) -> p h d", d=DH), ALU.add)
                        last.then_inc(v_copied, 1)
                    if s == 15 and live(*prv):
                        for t in range(KB):
                            bank = ps_any[:, bank_free(f"NAT{t}", i, k)[0]].rearrange(
                                "p t (h c) -> p (t h) c", c=32)
                            dve.wait_ge(nat_ready, count(*prv, 2, t + 1))
                            dve.wait_ge(p_self_done, count(*prv, 1, 1))
                            if (n := count(*prv, 2, t - 1)) is not None:
                                dve.wait_ge(attn_done, n)
                            nc.vector.tensor_tensor(den[:, t], bank[:, :, DH], p_self[:, t], ALU.add
                                                    ).then_inc(den_done, 1)
                            dve.wait_ge(den_done, count(*prv, 2, t + 1))
                            nc.vector.reciprocal(rden[:, t], den[:, t]).then_inc(rden_done, 1)
                            dve.wait_ge(vs_p_done, count(*prv, 1, 1))
                            dve.wait_ge(rden_done, count(*prv, 2, t + 1))
                            nc.vector.tensor_tensor(
                                num[:, t].rearrange("p (h d) -> p h d", d=DH), bank[:, :, 0:DH],
                                vs_p[:, t].rearrange("p (h d) -> p h d", d=DH), ALU.add).then_inc(num_done, 1)
                    if live(*b):
                        max_of(*b, s)
                if first:
                    weight_lo(3)
                    setup_pooling()
                if live(*b):
                    group_max(*b, 1)
                if live(*old):
                    dve.wait_ge(pool_p_done, count(*old, 2, 2))
                    kk = k - 2
                    rows_cnt = cnt[:].rearrange("p (i k) t -> p i k t", k=2)[:, i + kk // 2, kk % 2]
                    nc.vector.tensor_tensor(pool_den[:], pool_sum[:], rows_cnt, ALU.mult
                                            ).then_inc(pool_den_done, 1)
                    dve.wait_ge(pool_den_done, count(*old, 1, 1))
                    nc.vector.reciprocal(pool_r[:], pool_den[:]).then_inc(pool_r_done, 1)
                    dve.wait_ge(pool_r_done, count(*old, 1, 1))
                    dve.wait_ge(po_ready, count(*old, 1, 1))
                    if (n := count(*old, 16, 0)) is not None:
                        dve.wait_ge(out_stored, n)
                    for t in range(KB):
                        last = nc.vector.scalar_tensor_tensor(
                            out=o_out[:, t], in0=ps_any[:, bank_free("PO", i, k)[0], t],
                            scalar=pool_r[:, t:t + 1], in1=x1[:, t], op0=ALU.mult, op1=ALU.add)
                    last.then_inc(out_done, 1)

            weight_lo(0)
            for i, k in BEFORE:
                period(i, k)
            with dve.Fori(LOOP_FROM, LOOP_TO) as i:
                for k in BODY:
                    period(i, k)
            for i, k in AFTER:
                period(i, k)

        @block.tensor
        def _(pe):
            def products(out_of, hi, lo, n, stationary_w, halves=(0, 1)):
                for m in halves:
                    terms = [(kb, a, c) for kb in range(KB) for a, c in ((0, 0), (0, 1), (1, 0))]
                    for j, (kb, a, c) in enumerate(terms):
                        act_part, w_part = (hi, lo)[a], (w_hi, w_lo)[c]
                        if stationary_w:
                            lhs, rhs = w_part[:, n, kb, P * m:P * m + P], act_part[:, kb, :]
                        else:
                            lhs, rhs = act_part[:, kb, P * m:P * m + P], w_part[:, n, kb, :]
                        last = pe.matmul(out_of[:, m], lhs, rhs, start=(j == 0), stop=(j == len(terms) - 1))
                return last

            def transposed(out_of, src):
                for kb in range(KB):
                    for t in range(KB):
                        last = pe.transpose(out_of[:, kb, P * t:P * t + P], src[:, t, P * kb:P * kb + P], ident[:])
                return last

            def take_bank(step, i, k):
                bank, reader, n = bank_free(step, i, k)
                if n is not None:
                    pe.wait_ge(reader, n)
                return ps_any[:, bank]

            def score_for_max(i, k, h):
                par, e, j = k % 2, h % 2, h // 2
                if h % MG == 0:
                    pe.wait_ge(q_placed[h // MG], count(i, k, 32, 32))
                    pe.wait_ge(k_placed[h // MG], count(i, k, 48, 48))
                if (n := count(i, k, H, h - 1)) is not None:
                    pe.wait_ge(max_found, n)
                rows = slice(64 * e, 64 * e + KM)
                for t in range(KB):
                    last = pe.matmul(ps_max[:, e, t], q_rows[par][rows, j, P * t:P * t + P],
                                     k_rows[par][rows, j, :], start=True, stop=True)
                last.then_inc(max_scored, 1)

            def score_for_exp(i, k, h):
                par, e, j = k % 2, h % 2, h // 2
                if h % MG == 0:
                    pe.wait_ge(max_placed[h // MG], count(i, k, 32, 32))
                if (n := count(i, k, H, h - 1)) is not None:
                    pe.wait_ge(p_ready, n)
                rows = slice(64 * e, 64 * e + KF)
                for t in range(KB):
                    last = pe.matmul(ps_exp[:, e, t], k_rows[par][rows, j, P * t:P * t + P],
                                     q_rows[par][rows, j, :], start=True, stop=True)
                last.then_inc(scored, 1)

            def pv(i, k, g, pi, pk):
                par = k % 2
                bank = take_bank(f"PV{g}", pi, pk)
                pe.wait_ge(p_ready, count(i, k, H, GRP * (g + 1)))
                if g == 0:
                    pe.wait_ge(v_copied, count(i, k, 1, 1))
                for t in range(KB):
                    for c in range(GRP):
                        h = GRP * g + c
                        last = pe.matmul(bank[32 * c:32 * c + 32, 0, :], v_aug[par][:, t, h, :],
                                         pt[:, h % 8, t, :], start=(t == 0), stop=(t == KB - 1),
                                         skip_group_check=True)
                last.then_inc(pv_ready, 1)

            def max_to_rows(i, k, g, pi, pk):
                bank = take_bank(f"MT{g}", pi, pk)
                pe.wait_ge(neg_done, count(i, k, NM, g + 1))
                for t in range(KB):
                    last = pe.transpose(bank[0:4 * MJ, 0, P * t:P * t + P],
                                        neg_max[:, g, t].rearrange("p e c j -> p (e c j)"), ident[:])
                last.then_inc(mt_ready, 1)

            def biases():
                pe.wait_ge(bin_lo_done, 1)
                for n in range(2):
                    for m in range(2):
                        at = 8 * n + 4 * m
                        for j, (kb, part) in enumerate((kb, part) for kb in range(KB) for part in (w_hi, w_lo)):
                            last = pe.matmul(ps_max[:, 0, 0, at:at + 4], part[:, n, kb, P * m:P * m + P],
                                             bin_parts[:, kb].rearrange("p c b -> p (c b)"),
                                             start=(j == 0), stop=(j == 3))
                last.then_inc(bias_ready, 1)

            def self_scores(bank):
                by_block = bank[:, 0, 0:2 * H].rearrange("p (g t e j) -> p t e g j", g=NM, t=KB, e=2)
                for t in range(KB):
                    for e in range(2):
                        for part in (prod_hi, prod_lo):
                            last = pe.matmul(by_block[:, t, e], part[:, e, P * t:P * t + P], headsum[:],
                                             start=(part is prod_hi), stop=(part is prod_lo))
                return last

            def period(i, k):
                b, nxt, prv, old = (i, k), (i, k + 1), (i, k - 1), (i, k - 2)
                first = isinstance(i, int) and i < 0
                banks = {}
                for s in range(SLOTS):
                    if s == 1 and live(*prv):
                        max_to_rows(*prv, 1, i, k)
                    if s == 9 and live(*b):
                        max_to_rows(*b, 0, i, k)
                    if live(*b):
                        score_for_max(*b, s)
                    who = b if s >= LAG else prv
                    if live(*who):
                        score_for_exp(*who, (s - LAG) % SLOTS)
                    if s == 0 and live(*nxt):
                        bank = take_bank("TS", i, k)
                        pe.wait_ge(s_loaded[(k + 1) % 2], count(i + (k + 1) // 2, 0, 8, 16))
                        transposed(bank, s_sb[:, (k + 1) % 2]).then_inc(st_ready, 1)
                    if s % 4 == 0 and live(*prv):
                        pv(*prv, s // 4, i, k)
                    if live(*old):
                        if s == 1:
                            bank = take_bank("AT", i, k)
                            pe.wait_ge(attn_done, count(*old, 2, 2))
                            transposed(bank, attn).then_inc(at_ready, 1)
                        if s == 3:
                            bank = take_bank("WO", i, k)
                            pe.wait_ge(at_hi_done, count(*old, 1, 1))
                            pe.wait_ge(at_lo_done, count(*old, 1, 1))
                            if isinstance(i, int):
                                pe.wait_ge(w_lo_ready, 4)
                            products(bank, at_hi, at_lo, 3, False).then_inc(wo_ready, 1)
                        if s == 5:
                            bank = take_bank("X1T", i, k)
                            pe.wait_ge(x1_done, count(*old, 1, 1))
                            transposed(bank, x1).then_inc(x1t_ready, 1)
                        if s == 7:
                            bank = take_bank("Z", i, k)
                            pe.wait_ge(x1t_copied, count(*old, 1, 1))
                            if isinstance(i, int):
                                pe.wait_ge(consts_loaded, 6 * 16)
                            for kb in range(KB):
                                last = pe.matmul(bank[0:A, 0], w1[:, kb, :], x1t[:, kb, :],
                                                 start=(kb == 0), stop=(kb == KB - 1))
                            last.then_inc(z_ready, 1)
                        if s == 9:
                            bank = take_bank("SB", i, k)
                            pe.wait_ge(tanh_done, count(*old, 1, 1))
                            if isinstance(i, int):
                                pe.wait_ge(v_wide_ready, 1)
                            pe.matmul(bank[:, 0], v_wide[:], z_sb[:], start=True, stop=True).then_inc(sb_ready, 1)
                        if s == 12:
                            bank = take_bank("PT", i, k)
                            pe.wait_ge(pool_p_done, count(*old, 2, 2))
                            transposed(bank, pool_p).then_inc(pt_ready, 1)
                    if live(*nxt):
                        if s == 1:
                            bank = take_bank("TX", i, k)
                            pe.wait_ge(x_loaded[(k + 1) % 2], count(i + (k + 1) // 2, 0, 8, 16))
                            transposed(bank, x_sb[:, (k + 1) % 2]).then_inc(xt_ready, 1)
                        if s == 2:
                            bank = take_bank("Q", i, k)
                            pe.wait_ge(st_hi_done, count(*nxt, 1, 1))
                            pe.wait_ge(st_lo_done, count(*nxt, 1, 1))
                            if first:
                                pe.wait_ge(w_lo_ready, 1)
                            products(bank, st_hi, st_lo, 0, True).then_inc(q_ready, 1)
                        if s == 5:
                            banks["K"] = take_bank("K", i, k)
                            pe.wait_ge(xt_hi_done, count(*nxt, 1, 1))
                            pe.wait_ge(xt_lo_done, count(*nxt, 1, 1))
                            if first:
                                pe.wait_ge(w_lo_ready, 2)
                            products(banks["K"], xt_hi, xt_lo, 1, True, (0,))
                        if s == 6:
                            products(banks["K"], xt_hi, xt_lo, 1, True, (1,)).then_inc(k_ready, 1)
                            if first:
                                biases()
                            banks["KS"] = take_bank("KS", i, k)
                            products(banks["KS"], st_hi, st_lo, 1, True, (0,))
                        if s == 7:
                            products(banks["KS"], st_hi, st_lo, 1, True, (1,)).then_inc(ks_ready, 1)
                        if s == 9:
                            banks["VS"] = take_bank("VS", i, k)
                            if first:
                                pe.wait_ge(w_lo_ready, 3)
                            products(banks["VS"], st_hi, st_lo, 2, False, (0,))
                        if s == 10:
                            products(banks["VS"], st_hi, st_lo, 2, False, (1,)).then_inc(vs_ready, 1)
                            bank = take_bank("SS", i, k)
                            pe.wait_ge(prod_lo_done, count(*nxt, 1, 1))
                            if first:
                                pe.wait_ge(headsum_ready, 1)
                            self_scores(bank).then_inc(ss_ready, 1)
                        if s == 11:
                            banks["V"] = take_bank("V", i, k)
                            products(banks["V"], xt_hi, xt_lo, 2, False, (0,))
                        if s == 13:
                            products(banks["V"], xt_hi, xt_lo, 2, False, (1,)).then_inc(v_ready, 1)
                    if s == 14 and live(*prv):
                        for t in range(KB):
                            bank = take_bank(f"NAT{t}", i, k)
                            pe.wait_ge(pv_copied, count(*prv, NG, NG))
                            for gg in range(NG):
                                last = pe.transpose(bank[:, gg // 2, P * (gg % 2):P * (gg % 2) + P],
                                                    o_sb[:, gg, P * t:P * t + P], ident[:])
                            last.then_inc(nat_ready, 1)
                    if live(*old) and s in (14, 15):
                        t = s - 14
                        if t == 0:
                            banks["PO"] = take_bank("PO", i, k)
                            pe.wait_ge(pt_copied, count(*old, 1, 1))
                        for kb in range(KB):
                            last = pe.matmul(banks["PO"][:, t], pool_pt[:, kb, P * t:P * t + P], x1[:, kb, :],
                                             start=(kb == 0), stop=(kb == KB - 1))
                        if t == 1:
                            last.then_inc(po_ready, 1)

            pe.wait_ge(ident_ready, 1)

            for i, k in BEFORE:
                period(i, k)
            with pe.Fori(LOOP_FROM, LOOP_TO) as i:
                for k in BODY:
                    period(i, k)
            for i, k in AFTER:
                period(i, k)


_INS = ["x", "fside_BxSxS_0", "itok_B_18_1004", "itok_B_0_2", "L0_cond_Wq", "L0_cond_bq", "L0_cond_Wk",
        "L0_cond_bk", "L0_cond_Wv", "L0_cond_bv", "L0_cond_Wo", "L0_cond_bo", "L0_cond_b_prev",
        "L0_cond_b_self", "L1_cond_W1", "L1_cond_b1", "L1_cond_v"]


def kernel(**inputs):
    import numpy as _np
    import concourse.bacc as _bacc
    from concourse.bass_utils import run_bass_kernel_spmd as _run

    nc = _bacc.Bacc("TRN2", target_bir_lowering=False, num_devices=1)
    arrays, args = {}, []
    for name in _INS:
        a = _np.ascontiguousarray(inputs[name])
        arrays[f"in_{name}"] = a
        args.append(nc.dram_tensor(f"in_{name}", a.shape, mybir.dt.from_np(a.dtype), kind="ExternalInput").ap())
    out = nc.dram_tensor("out_0", inputs["x"].shape, F32, kind="ExternalOutput").ap()
    build(nc, *args, out)
    return _run(nc, [arrays], core_ids=[0]).results[0]["out_0"]
```
